# Optimizing a Trainium2 kernel written in Bass

```python
import numpy as np
import jax
import jax.numpy as jnp

def _softmax(x, axis=-1):
    return jax.nn.softmax(x, axis=axis)

def _gelu(x):
    return jax.nn.gelu(x, approximate=True)

def _silu(x):
    return jax.nn.silu(x)

def _sigmoid(x):
    return jax.nn.sigmoid(x)

def _layernorm(x, axis=-1, eps=1e-05):
    m = jnp.mean(x, axis=axis, keepdims=True)
    v = jnp.var(x, axis=axis, keepdims=True)
    return (x - m) / jnp.sqrt(v + eps)

def _scatter_add(tgt, idx, src, axis=0):
    return tgt.at[idx].add(src)

def _segment_sum(src, seg, n):
    return jax.ops.segment_sum(src, seg, n)
kernel_name = 'mk_cond_seq_d4_seqx_r8_1be322'

def setup_inputs(seed: int=0):
    np.random.seed(seed)
    _w = jnp.asarray

    def _rec_inputs():
        import jax
        import jax.numpy as jnp
        _rk = jax.random.key(seed)
        x = -7.109e-05 + 0.9999 * jax.random.normal(jax.random.fold_in(_rk, 1), (32, 32, 128), jnp.float32)
        _lenS = 32 - jax.random.randint(jax.random.fold_in(_rk, 7), (32,), 0, max(1, 32 // 4) + 1, jnp.int32)
        _lenS2 = 32 - jax.random.randint(jax.random.fold_in(_rk, 8), (32,), 0, max(1, 32 // 4) + 1, jnp.int32)
        itok_B_0_2 = jax.random.randint(jax.random.fold_in(_rk, 11), (32,), 0, 3, jnp.int32)
        itok_B_0_15 = jax.random.randint(jax.random.fold_in(_rk, 12), (32,), 0, 16, jnp.int32)
        condB_gatescore = jax.random.uniform(jax.random.fold_in(_rk, 13), (32,), jnp.float32, 0.0, 0.581427)
        condB_safetyscore = -0.927215 + 0.920279 * jax.random.normal(jax.random.fold_in(_rk, 14), (32,), jnp.float32)
        return (x, itok_B_0_2, itok_B_0_15, condB_gatescore, condB_safetyscore)
    x, itok_B_0_2, itok_B_0_15, condB_gatescore, condB_safetyscore = _rec_inputs()

    def _L0_cond_setup():
        import jax, jax.numpy as jnp
        import numpy as np
        H = 128
        EPS = 1e-05

        def _gelu(x):
            return jax.nn.gelu(x, approximate=False)
        key = jax.random.key(seed)
        ks = jax.random.split(key, 16)
        s = 1.0 / np.sqrt(H)
        inp = {'x': jax.random.normal(ks[0], (64, 128, H), dtype=jnp.float32), 'condition': jax.random.randint(ks[1], (64,), 0, 3), 'w1_nr': jax.random.normal(ks[2], (H, H), dtype=jnp.float32) * s, 'b1_nr': jnp.zeros((H,), dtype=jnp.float32), 'w2_nr': jax.random.normal(ks[3], (H, H), dtype=jnp.float32) * s, 'b2_nr': jnp.zeros((H,), dtype=jnp.float32), 'w1_tsr': jax.random.normal(ks[4], (H, H), dtype=jnp.float32) * s, 'b1_tsr': jnp.zeros((H,), dtype=jnp.float32), 'w2_tsr': jax.random.normal(ks[5], (H, H), dtype=jnp.float32) * s, 'b2_tsr': jnp.zeros((H,), dtype=jnp.float32), 'w1_sr': jax.random.normal(ks[6], (H, 2 * H), dtype=jnp.float32) * s, 'b1_sr': jnp.zeros((2 * H,), dtype=jnp.float32), 'w2_sr': jax.random.normal(ks[7], (2 * H, H), dtype=jnp.float32) * (1.0 / np.sqrt(2 * H)), 'b2_sr': jnp.zeros((H,), dtype=jnp.float32), 'w3_sr': jax.random.normal(ks[8], (H, H), dtype=jnp.float32) * s, 'b3_sr': jnp.zeros((H,), dtype=jnp.float32), 'gamma': jnp.ones((H,), dtype=jnp.float32), 'beta': jnp.zeros((H,), dtype=jnp.float32)}
        return inp
    _L0_cond_all = _L0_cond_setup()
    _L0_cond_in = {k: v for k, v in _L0_cond_all.items() if k in ('w1_nr', 'b1_nr', 'w2_nr', 'b2_nr', 'w1_tsr', 'b1_tsr', 'w2_tsr', 'b2_tsr', 'w1_sr', 'b1_sr', 'w2_sr', 'b2_sr', 'w3_sr', 'b3_sr', 'gamma', 'beta')}
    del _L0_cond_all

    def _L1_cond_setup():
        import jax, jax.numpy as jnp
        import numpy as np
        B, S, D = (32, 128, 128)
        A = 32
        E = 16
        LN_EPS = 1e-05
        key = jax.random.key(seed)
        ks = jax.random.split(key, 10)
        s = lambda fan_in: 1.0 / np.sqrt(fan_in)
        return {'hidden_states': jax.random.normal(ks[0], (B, S, D), dtype=jnp.float32), 'domain_id': jax.random.randint(ks[1], (B,), 0, E, dtype=jnp.int64), 'down_W': jax.random.uniform(ks[2], (A, D), jnp.float32, -s(D), s(D)), 'down_b': jax.random.uniform(ks[3], (A,), jnp.float32, -s(D), s(D)), 'up_W': jax.random.uniform(ks[4], (D, A), jnp.float32, -s(A), s(A)), 'up_b': jax.random.uniform(ks[5], (D,), jnp.float32, -s(A), s(A)), 'expert_W': jax.random.uniform(ks[6], (E, A, A), jnp.float32, -s(A), s(A)), 'expert_b': jax.random.uniform(ks[7], (E, A), jnp.float32, -s(A), s(A)), 'domain_emb': jax.random.normal(ks[8], (E, A), dtype=jnp.float32), 'ln_gamma': jnp.ones((D,), jnp.float32), 'ln_beta': jnp.zeros((D,), jnp.float32)}
    _L1_cond_all = _L1_cond_setup()
    _L1_cond_in = {k: v for k, v in _L1_cond_all.items() if k in ('down_W', 'down_b', 'up_W', 'up_b', 'expert_W', 'expert_b', 'domain_emb', 'ln_gamma', 'ln_beta')}
    del _L1_cond_all

    def _L2_cond_setup():
        import jax, jax.numpy as jnp
        import numpy as np
        D_MODEL = 128
        N_HEADS = 16
        D_HEAD = D_MODEL // N_HEADS
        D_FF = 512
        EPS = 1e-05

        def layernorm(x, gamma, beta):
            mu = jnp.mean(x, axis=-1, keepdims=True)
            var = jnp.var(x, axis=-1, keepdims=True)
            return (x - mu) * jax.lax.rsqrt(var + EPS) * gamma + beta
        key = jax.random.key(seed)
        ks = jax.random.split(key, 16)
        B, T = (4, 256)
        s = 1.0 / np.sqrt(D_MODEL)
        sf = 1.0 / np.sqrt(D_FF)
        return {'x': jax.random.normal(ks[0], (B, T, D_MODEL), jnp.float32), 'gate_score': jax.random.uniform(ks[1], (B,), jnp.float32), 'Wq': jax.random.normal(ks[2], (D_MODEL, D_MODEL), jnp.float32) * s, 'bq': jnp.zeros((D_MODEL,), jnp.float32), 'Wk': jax.random.normal(ks[3], (D_MODEL, D_MODEL), jnp.float32) * s, 'bk': jnp.zeros((D_MODEL,), jnp.float32), 'Wv': jax.random.normal(ks[4], (D_MODEL, D_MODEL), jnp.float32) * s, 'bv': jnp.zeros((D_MODEL,), jnp.float32), 'Wo': jax.random.normal(ks[5], (D_MODEL, D_MODEL), jnp.float32) * s, 'bo': jnp.zeros((D_MODEL,), jnp.float32), 'W1': jax.random.normal(ks[6], (D_MODEL, D_FF), jnp.float32) * s, 'b1': jnp.zeros((D_FF,), jnp.float32), 'W2': jax.random.normal(ks[7], (D_FF, D_MODEL), jnp.float32) * sf, 'b2': jnp.zeros((D_MODEL,), jnp.float32), 'gamma1': jnp.ones((D_MODEL,), jnp.float32), 'beta1': jnp.zeros((D_MODEL,), jnp.float32), 'gamma2': jnp.ones((D_MODEL,), jnp.float32), 'beta2': jnp.zeros((D_MODEL,), jnp.float32)}
    _L2_cond_all = _L2_cond_setup()
    _L2_cond_in = {k: v for k, v in _L2_cond_all.items() if k in ('Wq', 'bq', 'Wk', 'bk', 'Wv', 'bv', 'Wo', 'bo', 'W1', 'b1', 'W2', 'b2', 'gamma1', 'beta1', 'gamma2', 'beta2')}
    del _L2_cond_all

    def _L3_cond_setup():
        import jax, jax.numpy as jnp
        import numpy as np
        TEMPERATURE = 1.0
        ACT_THRESHOLD = 0.1
        MAX_ACT = 1.0
        SAFETY_KNOB = 1.0
        EPS = 1e-08

        def gram_schmidt(X):
            r = X.shape[1]
            Q = X
            for i in range(r):
                q = Q[:, i]
                q = q / (jnp.linalg.norm(q) + EPS)
                Q = Q.at[:, i].set(q)
                coeffs = q @ Q[:, i + 1:]
                Q = Q.at[:, i + 1:].add(-jnp.outer(q, coeffs))
            return Q
        key = jax.random.key(seed)
        ks = jax.random.split(key, 8)
        B, S, D, R = (8, 512, 128, 32)
        init_std = 0.02
        return {'hidden_states': jax.random.normal(ks[0], (B, S, D), jnp.float32), 'safety_score': jax.random.normal(ks[1], (B,), jnp.float32), 'U': jax.random.normal(ks[2], (D, R), jnp.float32) * init_std, 'V': jax.random.normal(ks[3], (D, R), jnp.float32) * init_std, 'safety_bias': jnp.zeros((D,), jnp.float32), 'gate_w1': jax.random.normal(ks[4], (D // 4, D), jnp.float32) * (1.0 / np.sqrt(D)), 'gate_b1': jnp.zeros((D // 4,), jnp.float32), 'gate_w2': jax.random.normal(ks[5], (1, D // 4), jnp.float32) * (1.0 / np.sqrt(D // 4)), 'gate_b2': jnp.zeros((1,), jnp.float32), 'resp_w': jax.random.normal(ks[6], (D, R), jnp.float32) * (1.0 / np.sqrt(R)), 'resp_b': jnp.zeros((D,), jnp.float32)}
    _L3_cond_all = _L3_cond_setup()
    _L3_cond_in = {k: v for k, v in _L3_cond_all.items() if k in ('U', 'V', 'safety_bias', 'gate_w1', 'gate_b1', 'gate_w2', 'gate_b2', 'resp_w', 'resp_b')}
    del _L3_cond_all
    return {'x': x, 'itok_B_0_2': itok_B_0_2, 'itok_B_0_15': itok_B_0_15, 'condB_gatescore': condB_gatescore, 'condB_safetyscore': condB_safetyscore, 'L0_cond_w1_nr': _L0_cond_in['w1_nr'], 'L0_cond_b1_nr': _L0_cond_in['b1_nr'], 'L0_cond_w2_nr': _L0_cond_in['w2_nr'], 'L0_cond_b2_nr': _L0_cond_in['b2_nr'], 'L0_cond_w1_tsr': _L0_cond_in['w1_tsr'], 'L0_cond_b1_tsr': _L0_cond_in['b1_tsr'], 'L0_cond_w2_tsr': _L0_cond_in['w2_tsr'], 'L0_cond_b2_tsr': _L0_cond_in['b2_tsr'], 'L0_cond_w1_sr': _L0_cond_in['w1_sr'], 'L0_cond_b1_sr': _L0_cond_in['b1_sr'], 'L0_cond_w2_sr': _L0_cond_in['w2_sr'], 'L0_cond_b2_sr': _L0_cond_in['b2_sr'], 'L0_cond_w3_sr': _L0_cond_in['w3_sr'], 'L0_cond_b3_sr': _L0_cond_in['b3_sr'], 'L0_cond_gamma': _L0_cond_in['gamma'], 'L0_cond_beta': _L0_cond_in['beta'], 'L1_cond_down_W': _L1_cond_in['down_W'], 'L1_cond_down_b': _L1_cond_in['down_b'], 'L1_cond_up_W': _L1_cond_in['up_W'], 'L1_cond_up_b': _L1_cond_in['up_b'], 'L1_cond_expert_W': _L1_cond_in['expert_W'], 'L1_cond_expert_b': _L1_cond_in['expert_b'], 'L1_cond_domain_emb': _L1_cond_in['domain_emb'], 'L1_cond_ln_gamma': _L1_cond_in['ln_gamma'], 'L1_cond_ln_beta': _L1_cond_in['ln_beta'], 'L2_cond_Wq': _L2_cond_in['Wq'], 'L2_cond_bq': _L2_cond_in['bq'], 'L2_cond_Wk': _L2_cond_in['Wk'], 'L2_cond_bk': _L2_cond_in['bk'], 'L2_cond_Wv': _L2_cond_in['Wv'], 'L2_cond_bv': _L2_cond_in['bv'], 'L2_cond_Wo': _L2_cond_in['Wo'], 'L2_cond_bo': _L2_cond_in['bo'], 'L2_cond_W1': _L2_cond_in['W1'], 'L2_cond_b1': _L2_cond_in['b1'], 'L2_cond_W2': _L2_cond_in['W2'], 'L2_cond_b2': _L2_cond_in['b2'], 'L2_cond_gamma1': _L2_cond_in['gamma1'], 'L2_cond_beta1': _L2_cond_in['beta1'], 'L2_cond_gamma2': _L2_cond_in['gamma2'], 'L2_cond_beta2': _L2_cond_in['beta2'], 'L3_cond_U': _L3_cond_in['U'], 'L3_cond_V': _L3_cond_in['V'], 'L3_cond_safety_bias': _L3_cond_in['safety_bias'], 'L3_cond_gate_w1': _L3_cond_in['gate_w1'], 'L3_cond_gate_b1': _L3_cond_in['gate_b1'], 'L3_cond_gate_w2': _L3_cond_in['gate_w2'], 'L3_cond_gate_b2': _L3_cond_in['gate_b2'], 'L3_cond_resp_w': _L3_cond_in['resp_w'], 'L3_cond_resp_b': _L3_cond_in['resp_b']}

def reference(x, itok_B_0_2, itok_B_0_15, condB_gatescore, condB_safetyscore, L0_cond_w1_nr, L0_cond_b1_nr, L0_cond_w2_nr, L0_cond_b2_nr, L0_cond_w1_tsr, L0_cond_b1_tsr, L0_cond_w2_tsr, L0_cond_b2_tsr, L0_cond_w1_sr, L0_cond_b1_sr, L0_cond_w2_sr, L0_cond_b2_sr, L0_cond_w3_sr, L0_cond_b3_sr, L0_cond_gamma, L0_cond_beta, L1_cond_down_W, L1_cond_down_b, L1_cond_up_W, L1_cond_up_b, L1_cond_expert_W, L1_cond_expert_b, L1_cond_domain_emb, L1_cond_ln_gamma, L1_cond_ln_beta, L2_cond_Wq, L2_cond_bq, L2_cond_Wk, L2_cond_bk, L2_cond_Wv, L2_cond_bv, L2_cond_Wo, L2_cond_bo, L2_cond_W1, L2_cond_b1, L2_cond_W2, L2_cond_b2, L2_cond_gamma1, L2_cond_beta1, L2_cond_gamma2, L2_cond_beta2, L3_cond_U, L3_cond_V, L3_cond_safety_bias, L3_cond_gate_w1, L3_cond_gate_b1, L3_cond_gate_w2, L3_cond_gate_b2, L3_cond_resp_w, L3_cond_resp_b):
    import jax
    import jax.numpy as jnp

    def _L0_cond_ref(x, condition, w1_nr, b1_nr, w2_nr, b2_nr, w1_tsr, b1_tsr, w2_tsr, b2_tsr, w1_sr, b1_sr, w2_sr, b2_sr, w3_sr, b3_sr, gamma, beta):
        import jax, jax.numpy as jnp
        import numpy as np
        H = 128
        EPS = 1e-05

        def _gelu(x):
            return jax.nn.gelu(x, approximate=False)
        out_nr = _gelu(jnp.einsum('bth,hk->btk', x, w1_nr) + b1_nr)
        out_nr = jnp.einsum('bth,hk->btk', out_nr, w2_nr) + b2_nr
        out_tsr = _gelu(jnp.einsum('bth,hk->btk', x, w1_tsr) + b1_tsr)
        out_tsr = jnp.einsum('bth,hk->btk', out_tsr, w2_tsr) + b2_tsr
        h = _gelu(jnp.einsum('bth,hk->btk', x, w1_sr) + b1_sr)
        h = _gelu(jnp.einsum('bth,hk->btk', h, w2_sr) + b2_sr)
        out_sr = jnp.einsum('bth,hk->btk', h, w3_sr) + b3_sr
        c = condition[:, None, None]
        out = jnp.where(c == 0, out_nr, jnp.where(c == 1, out_tsr, jnp.where(c == 2, out_sr, jnp.zeros_like(x))))
        y = x + out
        mu = jnp.mean(y, axis=-1, keepdims=True)
        var = jnp.mean((y - mu) ** 2, axis=-1, keepdims=True)
        return (y - mu) * jax.lax.rsqrt(var + EPS) * gamma + beta

    def _L1_cond_ref(hidden_states, domain_id, down_W, down_b, up_W, up_b, expert_W, expert_b, domain_emb, ln_gamma, ln_beta):
        import jax, jax.numpy as jnp
        import numpy as np
        B, S, D = (32, 128, 128)
        A = 32
        E = 16
        LN_EPS = 1e-05
        residual = hidden_states
        hidden = jnp.einsum('bsd,ad->bsa', hidden_states, down_W) + down_b
        hidden = jax.nn.gelu(hidden, approximate=False)
        valid = (domain_id >= 0) & (domain_id < E)
        idx = jnp.clip(domain_id, 0, E - 1)
        Wsel = expert_W[idx]
        bsel = expert_b[idx]
        expert_out = jnp.einsum('bsa,boa->bso', hidden, Wsel) + bsel[:, None, :]
        domain_output = jnp.where(valid[:, None, None], expert_out, hidden)
        hidden = domain_output + domain_emb[idx][:, None, :]
        hidden = jnp.einsum('bsa,da->bsd', hidden, up_W) + up_b
        x = hidden + residual
        mu = jnp.mean(x, axis=-1, keepdims=True)
        var = jnp.mean(jnp.square(x - mu), axis=-1, keepdims=True)
        return (x - mu) * jax.lax.rsqrt(var + LN_EPS) * ln_gamma + ln_beta

    def _L2_cond_ref(x, gate_score, Wq, bq, Wk, bk, Wv, bv, Wo, bo, W1, b1, W2, b2, gamma1, beta1, gamma2, beta2):
        import jax, jax.numpy as jnp
        import numpy as np
        D_MODEL = 128
        N_HEADS = 16
        D_HEAD = D_MODEL // N_HEADS
        D_FF = 512
        EPS = 1e-05

        def layernorm(x, gamma, beta):
            mu = jnp.mean(x, axis=-1, keepdims=True)
            var = jnp.var(x, axis=-1, keepdims=True)
            return (x - mu) * jax.lax.rsqrt(var + EPS) * gamma + beta
        B, T, C = x.shape
        h = layernorm(x, gamma1, beta1)
        Q = (h @ Wq + bq).reshape(B, T, N_HEADS, D_HEAD).transpose(0, 2, 1, 3)
        K = (h @ Wk + bk).reshape(B, T, N_HEADS, D_HEAD).transpose(0, 2, 1, 3)
        V = (h @ Wv + bv).reshape(B, T, N_HEADS, D_HEAD).transpose(0, 2, 1, 3)
        scores = jnp.einsum('bhqd,bhkd->bhqk', Q, K) / np.sqrt(D_HEAD)
        causal = jnp.tril(jnp.ones((T, T), dtype=bool))
        scores = jnp.where(causal, scores, -jnp.inf)
        attn = jax.nn.softmax(scores, axis=-1)
        ctx = jnp.einsum('bhqk,bhkd->bhqd', attn, V)
        ctx = ctx.transpose(0, 2, 1, 3).reshape(B, T, C)
        attn_out = ctx @ Wo + bo
        x1 = x + attn_out
        h2 = layernorm(x1, gamma2, beta2)
        ff = jax.nn.gelu(h2 @ W1 + b1, approximate=False) @ W2 + b2
        x2 = x1 + ff
        g = gate_score[:, None, None]
        return x + g * (x2 - x)

    def _L3_cond_ref(hidden_states, safety_score, U, V, safety_bias, gate_w1, gate_b1, gate_w2, gate_b2, resp_w, resp_b):
        import jax, jax.numpy as jnp
        import numpy as np
        TEMPERATURE = 1.0
        ACT_THRESHOLD = 0.1
        MAX_ACT = 1.0
        SAFETY_KNOB = 1.0
        EPS = 1e-08

        def gram_schmidt(X):
            r = X.shape[1]
            Q = X
            for i in range(r):
                q = Q[:, i]
                q = q / (jnp.linalg.norm(q) + EPS)
                Q = Q.at[:, i].set(q)
                coeffs = q @ Q[:, i + 1:]
                Q = Q.at[:, i + 1:].add(-jnp.outer(q, coeffs))
            return Q
        R = resp_w.shape[1]
        U_o = gram_schmidt(U)
        V_o = gram_schmidt(V)
        basis = U_o @ V_o.T
        pooled = hidden_states.mean(axis=1)
        h1 = jax.nn.relu(pooled @ gate_w1.T + gate_b1)
        base_act = jax.nn.sigmoid(h1 @ gate_w2.T + gate_b2)
        mod = jax.nn.sigmoid(safety_score[:, None] / TEMPERATURE)
        knob = jnp.clip(jnp.asarray(SAFETY_KNOB, hidden_states.dtype), ACT_THRESHOLD, MAX_ACT)
        strength = (base_act * mod * knob)[:, None, :]
        proj = hidden_states @ basis
        feats = proj @ basis.T[:, :R]
        response = feats @ resp_w.T + resp_b + safety_bias
        return hidden_states + strength * response
    x = _L0_cond_ref(x, itok_B_0_2, L0_cond_w1_nr, L0_cond_b1_nr, L0_cond_w2_nr, L0_cond_b2_nr, L0_cond_w1_tsr, L0_cond_b1_tsr, L0_cond_w2_tsr, L0_cond_b2_tsr, L0_cond_w1_sr, L0_cond_b1_sr, L0_cond_w2_sr, L0_cond_b2_sr, L0_cond_w3_sr, L0_cond_b3_sr, L0_cond_gamma, L0_cond_beta)
    x = _L1_cond_ref(x, itok_B_0_15, L1_cond_down_W, L1_cond_down_b, L1_cond_up_W, L1_cond_up_b, L1_cond_expert_W, L1_cond_expert_b, L1_cond_domain_emb, L1_cond_ln_gamma, L1_cond_ln_beta)
    x = _L2_cond_ref(x, condB_gatescore, L2_cond_Wq, L2_cond_bq, L2_cond_Wk, L2_cond_bk, L2_cond_Wv, L2_cond_bv, L2_cond_Wo, L2_cond_bo, L2_cond_W1, L2_cond_b1, L2_cond_W2, L2_cond_b2, L2_cond_gamma1, L2_cond_beta1, L2_cond_gamma2, L2_cond_beta2)
    x = _L3_cond_ref(x, condB_safetyscore, L3_cond_U, L3_cond_V, L3_cond_safety_bias, L3_cond_gate_w1, L3_cond_gate_b1, L3_cond_gate_w2, L3_cond_gate_b2, L3_cond_resp_w, L3_cond_resp_b)
    return x

_drawn_inputs = setup_inputs


def setup_inputs(seed=0):
    import zlib

    import numpy as np

    out = dict(_drawn_inputs(seed))
    spreads = {'L0_cond_b1_nr': (0.0, 0.267),
     'L0_cond_b2_nr': (0.0, 0.1),
     'L0_cond_b1_tsr': (0.0, 0.1),
     'L0_cond_b2_tsr': (0.0, 0.1),
     'L0_cond_b1_sr': (0.0, 0.397),
     'L0_cond_b2_sr': (0.0, 0.1),
     'L0_cond_b3_sr': (0.0, 0.1),
     'L0_cond_gamma': (1.0, 0.2),
     'L0_cond_beta': (0.0, 0.1),
     'L1_cond_ln_gamma': (1.0, 0.2),
     'L1_cond_ln_beta': (0.0, 0.1),
     'L2_cond_bq': (0.0, 0.78),
     'L2_cond_bk': (0.0, 2.0),
     'L2_cond_bv': (0.0, 0.1),
     'L2_cond_bo': (0.0, 0.1),
     'L2_cond_b1': (0.0, 0.339),
     'L2_cond_b2': (0.0, 0.1),
     'L2_cond_gamma1': (1.0, 0.2),
     'L2_cond_beta1': (0.0, 0.1),
     'L2_cond_gamma2': (1.0, 0.2),
     'L2_cond_beta2': (0.0, 0.317),
     'L3_cond_safety_bias': (0.0, 0.41),
     'L3_cond_gate_b1': (0.0, 0.8),
     'L3_cond_resp_b': (0.0, 0.454)}
    factors = {'L1_cond_down_b': 5.803, 'L3_cond_V': 64.0, 'L3_cond_gate_w1': 4.025}
    for name, (base, spread) in spreads.items():
        noise = np.random.default_rng([zlib.crc32(name.encode()), seed]).standard_normal(out[name].shape)
        drawn = base * np.exp(spread * noise) if base else spread * noise
        out[name] = jnp.asarray(drawn.astype(out[name].dtype))
    for name, factor in factors.items():
        out[name] = (out[name] * factor).astype(out[name].dtype)
    return out
```

```python
from contextlib import ExitStack

import numpy as np
import concourse.bass as bass
from concourse import mybir

F32 = mybir.dt.float32
BF16 = mybir.dt.bfloat16
F16 = mybir.dt.float16
I32 = mybir.dt.int32
ALU = mybir.AluOpType
ACT = mybir.ActivationFunctionType
AX = mybir.AxisListType

P = 128
S = 32
B = 32
NH = 16
DH = P // NH
A = 32
E = 16
EX = E + 2
R = 32
Q = 4
NT = 2
HT = B * S // NT
HB = B // NT
FF = 4
HD = A + Q
EPS = 1e-5
GS_EPS = 1e-8
OFF = -1e9
MASKED = -1e30

COLS = ["b1_nr", "b1_tsr", "b1_sr0", "b1_sr1", "b2_sr", "gamma0", "beta0", "down_b",
        "gamma2a", "beta2a", "bq", "bk", "bv", "gamma2", "beta2", "f0", "f1", "f2", "f3",
        "gate_b1", "gate_w2", "gate_b2", "expert_id"] + \
       [f"gate{c}" for c in range(8)] + [f"safety{c}" for c in range(8)]
COL = {n: i for i, n in enumerate(COLS)}
ROWS = ["gamma0", "beta0", "up_b", "gamma1", "beta1", "bo", "b2", "resp_b", "safety_bias"]
ROW = {n: i for i, n in enumerate(ROWS)}


def build(nc, src, out_dram):
    with ExitStack() as ctx:
        def sb(name, cols, dt=F32, rows=P):
            return ctx.enter_context(nc.sbuf_tensor(name, [rows, cols], dt))

        def sem(name):
            return ctx.enter_context(nc.semaphore(name))

        def view(t, off, dims, p0=0, rows=P):
            a = t[p0:p0 + rows, off:off + 1]
            return bass.AP(a.tensor, a.offset, [list(a.ap[0])] + [list(d) for d in dims])

        xF = sb("xF", NT * HT)
        xT = sb("xT", NT * HT)
        w0 = sb("w0", 9 * P)
        col = sb("col", len(COLS))
        rows = sb("rows", len(ROWS) * P)
        w1 = sb("w1", A + Q * P + A)
        w2 = sb("w2", 4 * P)
        w3 = sb("w3", 2 * FF * P)
        uv = sb("uv", P, rows=2 * R)
        respw = sb("respw", P, rows=R)
        expw = sb("expw", A * A, rows=EX)
        expbe = sb("expbe", 2 * P, rows=EX)
        ids_i = sb("ids_i", B, I32, rows=EX)
        cond_i = sb("cond_i", B, I32, rows=3)
        b2c = sb("b2c", P, rows=3)
        ident = sb("ident", P)
        gsneg = sb("gsneg", R, rows=2 * R)
        gsdiag = sb("gsdiag", R, rows=2 * R)
        headmask = sb("headmask", Q)
        keymask = sb("keymask", Q)
        cidx = sb("cidx", 1, rows=3)
        identb = sb("identb", P, BF16)
        maskl = sb("maskl", P, BF16)
        maskr = sb("maskr", S, BF16)
        offb = sb("offb", 3, BF16, rows=3)

        ids = sb("ids", B, rows=EX)
        onehot = sb("onehot", B, rows=EX)
        condf = sb("condf", B, rows=3)
        chosen = sb("chosen", B * S, rows=3)
        other = sb("other", B, BF16, rows=3)
        half_neg = sb("half_neg", 8)
        half_pos = sb("half_pos", 1, rows=2 * R)
        expbd = sb("expbd", NT * Q * P)
        expb = sb("expb", NT * Q)
        b0u = sb("b0u", P)
        rsb = sb("rsb", P)
        hnr = [sb(f"hnr{t}", HT) for t in range(NT)]
        htsr = [sb(f"htsr{t}", HT) for t in range(NT)]
        hsr = [sb(f"hsr{t}", 2 * HT) for t in range(NT)]
        zsr = [sb(f"zsr{t}", HT) for t in range(NT)]
        y = [sb(f"y{t}", HT) for t in range(NT)]
        n = [sb(f"n{t}", HT) for t in range(NT)]
        st = sb("st", NT * Q * 6)
        mv = sb("mv", NT * Q * 2)
        ve = sb("ve", NT * Q)
        rstd = sb("rstd", NT * Q)
        aF = [sb(f"aF{t}", HT) for t in range(NT)]
        a0T = [sb(f"a0T{t}", HT) for t in range(NT)]
        tmp = [sb(f"tmp{t}", HT) for t in range(NT)]
        hid = [sb(f"hid{t}", P) for t in range(NT)]
        hid2 = [sb(f"hid2{t}", P) for t in range(NT)]
        a1T = [sb(f"a1T{t}", HT) for t in range(NT)]
        hF = [sb(f"hF{t}", HT) for t in range(NT)]
        q32, k32 = hnr, htsr
        qh = [sb(f"qh{t}", HT, F16) for t in range(NT)]
        ql = [sb(f"ql{t}", HT, F16) for t in range(NT)]
        kh = [sb(f"kh{t}", HT, F16) for t in range(NT)]
        kl = [sb(f"kl{t}", HT, F16) for t in range(NT)]
        qbh = [sb(f"qbh{t}", Q * HT, F16) for t in range(NT)]
        qbl = [sb(f"qbl{t}", Q * HT, F16) for t in range(NT)]
        vbd = [sb(f"vbd{t}", HB * Q * HD) for t in range(NT)]
        mx = [sb(f"mx{t}", Q * HB, BF16) for t in range(NT)]
        ex = [sb(f"ex{t}", Q * HT) for t in range(NT)]
        exT = [sb(f"exT{t}", Q * HT) for t in range(NT)]
        rden = [sb(f"rden{t}", Q * NH) for t in range(NT)]
        cT = [sb(f"cT{t}", HT) for t in range(NT)]
        cF = [sb(f"cF{t}", HT) for t in range(NT)]
        x1 = [sb(f"x1{t}", HT) for t in range(NT)]
        a1bo = [sb(f"a1bo{t}", HT) for t in range(NT)]
        xd = [sb(f"xd{t}", HT) for t in range(NT)]
        fF = hF
        g = ex
        oT = [sb(f"oT{t}", HT) for t in range(NT)]
        oF = cF
        pool_s = [sb(f"pool{t}", HB) for t in range(NT)]
        h1 = [sb(f"h1{t}", HT, rows=R) for t in range(NT)]
        gb2h = sb("gb2h", 1)
        sact = sb("sact", 8)
        smod = sb("smod", 8)
        smod4 = sb("smod4", 8)
        stren = sb("stren", 8)
        res = y
        gsq = sb("gsq", P, rows=2 * R)
        gsjunk = sb("gsjunk", P, rows=2 * R)
        gsn2 = sb("gsn2", R, rows=2 * R)
        gsn = sb("gsn", R, rows=2 * R)
        gsne = sb("gsne", R, rows=2 * R)
        gsr = sb("gsr", R, rows=2 * R)
        gsc = sb("gsc", R, rows=2 * R)
        gsf = sb("gsf", R, rows=2 * R)
        gsd = sb("gsd", R + 1, rows=2 * R)
        uo = sb("uo", P, rows=R)
        vo = sb("vo", P, rows=R)
        basisT = sb("basisT", P)
        basisR = sb("basisR", P, rows=R)
        t2 = sb("t2", P)
        m3 = sb("m3", P)

        S_ = [ctx.enter_context(nc.psum_tensor(f"S{i}", [P, 512], F32)) for i in range(4)]
        B0 = ctx.enter_context(nc.psum_tensor("B0", [P, 512], F32))
        B1 = ctx.enter_context(nc.psum_tensor("B1", [P, 512], F32))
        B2 = ctx.enter_context(nc.psum_tensor("B2", [P, 512], F32))
        G = ctx.enter_context(nc.psum_tensor("G", [P, 512], F32))

        ld = {k: sem("ld_" + k) for k in ("small", "x0", "x1", "xT", "w0", "rows", "w1", "w2",
                                          "w3", "gs", "expert")}
        s = {k: sem(k) for k in (
            "ids_ready", "onehot_ready", "chosen_ready", "expert_picked", "expbd_ready",
            "zeroed", "halves_ready", "rowsums_ready", "vones_ready", "ids_step",
            "pre_nr", "pre_tsr", "pre_sr0", "pre_sr1", "h_ready", "pre_z", "z_ready", "y0_ready",
            "y0_sum", "y1_sum", "x1_ready", "stats", "mv_ready", "ve_ready", "rstd_ready",
            "n0_ready", "n1_ready", "nq_ready", "nf_ready", "a0_tmp", "a0T_ready",
            "aF_pre", "aF_ready", "hF_pre", "hF_ready", "fF_pre", "fF_ready",
            "hid_pre", "hid_ready", "hid2_pre", "hid2_ready", "up_ready", "a1_tmp", "a1_ready",
            "q_pre", "k_pre", "q_ready", "k_ready", "qh_ready", "kh_ready", "ql_ready", "qk_split",
            "v_pre", "v_ready", "s_ready", "mx_ready", "s_sub", "ex_ready", "exT_ready",
            "pv_ready", "rden_ready", "ctx_ready", "cF_pre", "cF_ready", "wo_ready",
            "a1bo_ready", "xd_tmp", "xd_ready",
            "ff_pre", "g_ready", "ff_ready", "u_ready", "o_ready", "oF_pre", "oF_ready",
            "pooled", "h1_pre", "h1_ready", "gate_pre", "gate_act", "mod_ready", "stren_step",
            "stren_ready", "resp_ready", "r_ready", "res_ready", "stored", "gb_ready",
            "gs_q", "gs_sq", "gs_n", "gs_ne", "gs_c", "gs_rec", "gs_f", "gs_col",
            "gs_d", "gs_uv", "gs_m", "gs_mc",
        )}

        def stepper(one):
            state = [0]

            def gs(k=1):
                for _ in range(k):
                    if state[0] < R:
                        one(state[0])
                        state[0] += 1
            return gs

        block = ctx.enter_context(nc.Block())

        @block.sync
        def _(sp):
            def load(dst, what, key):
                sp.dma_start(dst, src[what]).then_inc(ld[key], 16)
            load(cond_i[:], "cond", "small")
            load(ids_i[:], "ids", "small")
            load(col[:], "col", "small")
            load(b2c[:], "b2c", "small")
            load(keymask[:], "keymask", "small")
            load(cidx[:], "cidx", "small")
            load(offb[:], "offb", "small")
            load(w0[:, 0:4 * P], "w0a", "w0")
            load(xF[:, 0:HT], "xFa", "x0")
            load(expw[:], "expw", "expert")
            load(expbe[:], "expbe", "expert")
            load(uv[:], "uv", "gs")
            load(gsneg[:], "gsneg", "gs")
            load(gsdiag[:], "gsdiag", "gs")
            load(ident[:], "ident", "gs")
            load(w0[:, 4 * P:9 * P], "w0b", "w0")
            load(xF[:, HT:2 * HT], "xFb", "x1")
            load(xT[:, 0:HT], "xTa", "xT")
            load(xT[:, HT:2 * HT], "xTb", "xT")
            load(rows[:], "rows", "rows")
            load(w1[:], "w1", "w1")
            load(w2[:], "w2", "w2")
            load(identb[:], "identb", "w2")
            load(maskl[:], "maskl", "w2")
            load(maskr[:], "maskr", "w2")
            load(headmask[:], "headmask", "w2")
            load(w3[:], "w3", "w3")
            load(respw[:], "respw", "w3")
            for t in range(NT):
                sp.wait_ge(s["res_ready"], t + 1)
                sp.dma_start(out_dram[:, t * HT:(t + 1) * HT], res[t][:]).then_inc(s["stored"], 16)
            sp.wait_ge(s["stored"], 16 * NT)

        @block.tensor
        def _(pe):
            mm = nc.tensor.matmul

            def gs_step(i):
                if i == 0:
                    pe.wait_ge(ld["gs"], 64)
                    pe.wait_ge(s["expbd_ready"], 5)
                else:
                    pe.wait_ge(s["gs_col"], i)
                for k in range(2):
                    half = slice(k * R, (k + 1) * R)
                    j = mm(G[half, 0:P], view(ident, k * R + i, [(0, R)], k * R, R), uv[half, :],
                           start=True, stop=True)
                j.then_inc(s["gs_q"], 1)

            gs = stepper(gs_step)

            pe.wait_ge(ld["expert"], 32)
            pe.wait_ge(s["onehot_ready"], 1)
            for o8 in range(A // Q):
                mm(G[:, B * o8:B * o8 + B], expw[:, o8 * P:(o8 + 1) * P], onehot[:],
                   start=True, stop=True)
            for k in range(2):
                i = mm(G[:, 256:256 + B], expbe[:, k * P:(k + 1) * P], onehot[:],
                       start=(k == 0), stop=(k == 1))
            i.then_inc(s["expert_picked"], 1)

            def L0_first(t):
                if t == 0:
                    pe.wait_ge(ld["w0"], 16)
                    pe.wait_ge(ld["x0"], 16)
                    pe.wait_ge(s["chosen_ready"], 2)
                else:
                    pe.wait_ge(ld["x1"], 16)
                x = xF[:, t * HT:(t + 1) * HT]
                for k, name in enumerate(("pre_nr", "pre_tsr", "pre_sr0", "pre_sr1")):
                    if t == 1:
                        pe.wait_ge(s["h_ready"], k + 1)
                    i = mm(S_[k][:], w0[:, k * P:(k + 1) * P], x, start=True, stop=(k > 1),
                           skip_group_check=True)
                    if k < 2:
                        i = mm(S_[k][:], view(offb, k, [(0, P)], rows=3),
                               view(other, t * HB, [(1, HB), (0, S)], rows=3),
                               start=False, stop=True, skip_group_check=True)
                    i.then_inc(s[name], 1)

            def L0_second(t):
                if t == 0:
                    pe.wait_ge(ld["w0"], 32)
                pe.wait_ge(s["h_ready"], 4 * t + 4)
                if t == 1:
                    pe.wait_ge(s["z_ready"], 1)
                mm(B0[:], view(offb, 2, [(0, P)], rows=3),
                   view(other, t * HB, [(1, HB), (0, S)], rows=3), start=True, stop=False,
                   skip_group_check=True)
                for k in range(2):
                    i = mm(B0[:], w0[:, (6 + k) * P:(7 + k) * P], hsr[t][:, k * HT:(k + 1) * HT],
                           start=False, stop=(k == 1), skip_group_check=True)
                i.then_inc(s["pre_z"], 1)

            def L0_third(t):
                if t == 1:
                    pe.wait_ge(s["y0_sum"], 1)
                for c in range(Q):
                    tok = slice(c * P, (c + 1) * P)
                    o = B1[:, tok]
                    mm(o, chosen[:, (t * Q + c) * P:(t * Q + c + 1) * P], b2c[:],
                       start=(c == 0), stop=False, skip_group_check=True)
                    mm(o, hnr[t][:, tok], w0[:, 4 * P:5 * P], start=False, stop=False,
                       skip_group_check=True)
                    mm(o, htsr[t][:, tok], w0[:, 5 * P:6 * P], start=False, stop=False,
                       skip_group_check=True)
                for c in range(Q):
                    if c == 0:
                        pe.wait_ge(s["z_ready"], t + 1)
                    tok = slice(c * P, (c + 1) * P)
                    i = mm(B1[:, tok], zsr[t][:, tok], w0[:, 8 * P:9 * P], start=False, stop=True,
                           skip_group_check=True)
                i.then_inc(s["y0_ready"], 1)

            def to_F(source, waits, signal):
                for name, value in waits:
                    pe.wait_ge(s[name], value)
                for c in range(Q):
                    i = nc.tensor.transpose(B2[:, c * P:(c + 1) * P], source[:, c * P:(c + 1) * P],
                                            ident[:])
                i.then_inc(s[signal], 1)

            def L1_down(t):
                if t == 0:
                    pe.wait_ge(ld["w1"], 16)
                pe.wait_ge(s["aF_ready"], t + 1)
                for c in range(Q):
                    i = mm(S_[t][c * A:(c + 1) * A, 0:P], w1[:, 0:A], aF[t][:, c * P:(c + 1) * P],
                           start=True, stop=True)
                i.then_inc(s["hid_pre"], 1)

            def L1_expert(t):
                pe.wait_ge(s["hid_ready"], t + 1)
                if t == 0:
                    pe.wait_ge(s["expbd_ready"], 5)
                for j in range(Q):
                    sl = slice(j * S, (j + 1) * S)
                    at = (t * Q + j) * P
                    i = mm(S_[2 + t][:, sl], expbd[:, at:at + P], hid[t][:, sl],
                           start=True, stop=True)
                i.then_inc(s["hid2_pre"], 1)

            def L1_up(t):
                pe.wait_ge(s["hid2_ready"], t + 1)
                pe.wait_ge(*((s["y0_sum"], 2) if t == 0 else (s["y1_sum"], 1)))
                mm(B1[:], hid2[t][:], w1[:, A:A + Q * P], start=True, stop=True)\
                    .then_inc(s["up_ready"], 1)

            def qkv(t):
                if t == 0:
                    pe.wait_ge(ld["w2"], 80)
                pe.wait_ge(s["hF_ready"], t + 1)
                if t == 1:
                    pe.wait_ge(s["q_ready"], 1)
                mm(B0[:], w2[:, 0:P], hF[t][:], start=True, stop=True).then_inc(s["q_pre"], 1)
                if t == 0:
                    pe.wait_ge(s["y1_sum"], 2)
                else:
                    pe.wait_ge(s["k_ready"], 1)
                mm(B1[:], w2[:, P:2 * P], hF[t][:], start=True, stop=True).then_inc(s["k_pre"], 1)

            def values(t):
                if t == 1:
                    pe.wait_ge(s["ex_ready"], 2)
                for b in range(HB):
                    for h in range(Q):
                        i = mm(S_[t][h * S:(h + 1) * S, b * A:(b + 1) * A],
                               hF[t][:, b * S:(b + 1) * S],
                               view(w2, 2 * P + h * DH, [(A, Q), (1, DH)]), start=True, stop=True)
                i.then_inc(s["v_pre"], 1)

            def scores(t):
                pe.wait_ge(s["qk_split"], t + 1)
                for r in range(Q):
                    rows_ = slice(r * A, (r + 1) * A)
                    if t == 0:
                        pe.wait_ge(s["v_ready"], 4)
                    else:
                        pe.wait_ge(s["v_ready"], 8)
                        pe.wait_ge(s["ex_ready"], r + 1)
                    mm(S_[r][:], maskl[rows_, :], view(maskr, 0, [(0, HB), (1, S)], r * A, A),
                       start=True, stop=False, skip_group_check=True)
                    for b in range(HB):
                        qs = qbh[t][rows_, b * P:(b + 1) * P]
                        qsl = qbl[t][rows_, b * P:(b + 1) * P]
                        sl = slice(b * S, (b + 1) * S)
                        o = S_[r][:, sl]
                        mm(o, qs, kh[t][rows_, sl], start=False, stop=False, skip_group_check=True)
                        mm(o, qs, kl[t][rows_, sl], start=False, stop=False, skip_group_check=True)
                        i = mm(o, qsl, kh[t][rows_, sl], start=False, stop=(b == HB - 1),
                               skip_group_check=True)
                    i.then_inc(s["s_ready"], 1)

            def subtract(t, r):
                pe.wait_ge(s["mx_ready"], 4 * t + r + 1)
                mm(S_[r][:], identb[:], view(mx[t], r * HB, [(1, HB), (0, S)]),
                   start=False, stop=True, skip_group_check=True).then_inc(s["s_sub"], 1)

            def context(t):
                pe.wait_ge(s["v_ready"], 4 * t + 4)
                if t == 0:
                    pe.wait_ge(s["vones_ready"], 2)
                pe.wait_ge(s["k_ready"], 2)
                if t == 1:
                    pe.wait_ge(s["x1_ready"], 1)
                for r in range(Q):
                    pe.wait_ge(s["exT_ready"], 4 * t + r + 1)
                    for b in range(HB):
                        c, j = divmod(b, Q)
                        bank = (B0, B1)[c // 2]
                        at = (c % 2) * Q * HD + r * HD
                        i = mm(bank[j * S:(j + 1) * S, at:at + HD],
                               exT[t][:, r * HT + b * S:r * HT + (b + 1) * S],
                               vbd[t][:, (b * Q + r) * HD:(b * Q + r + 1) * HD],
                               start=True, stop=True, skip_group_check=True)
                i.then_inc(s["pv_ready"], 1)

            def wo(t):
                pe.wait_ge(s["cF_ready"], t + 1)
                pe.wait_ge(s["ctx_ready"], 2 * t + 2)
                for c in range(Q):
                    sl = slice(c * P, (c + 1) * P)
                    i = mm(B0[:, sl], cF[t][:, sl], w2[:, 3 * P:4 * P], start=True, stop=True)
                i.then_inc(s["wo_ready"], 1)

            def ff_in(t):
                if t == 0:
                    pe.wait_ge(ld["w3"], 32)
                pe.wait_ge(s["fF_ready"], t + 1)
                for k in range(FF):
                    if t == 0:
                        pe.wait_ge(s["ex_ready"], 8)
                    else:
                        pe.wait_ge(s["g_ready"], k + 1)
                    mm(S_[k][:], w3[:, k * P:(k + 1) * P], fF[t][:], start=True, stop=True)\
                        .then_inc(s["ff_pre"], 1)

            def ff_out(t):
                if t == 0:
                    pe.wait_ge(s["ctx_ready"], 4)
                else:
                    pe.wait_ge(s["u_ready"], 1)
                for k in range(FF):
                    pe.wait_ge(s["g_ready"], 4 * t + k + 1)
                    for c in range(Q):
                        i = mm(B1[:, c * P:(c + 1) * P],
                               g[t][:, k * HT + c * P:k * HT + (c + 1) * P],
                               w3[:, (FF + k) * P:(FF + k + 1) * P],
                               start=(k == 0 and c == 0), stop=(k == FF - 1), skip_group_check=True)
                i.then_inc(s["ff_ready"], 1)

            def gate(t):
                pe.wait_ge(s["pooled"], t + 1)
                if t == 1:
                    pe.wait_ge(s["gate_act"], 1)
                mm(G[0:R, 0:HB], w1[:, A + Q * P:A + Q * P + R], pool_s[t][:], start=True, stop=True)\
                    .then_inc(s["h1_pre"], 1)

            def gate2(t):
                pe.wait_ge(s["h1_ready"], t + 1)
                for c in range(Q):
                    i = mm(G[:, c:c + 1], h1[t][:, c * P:(c + 1) * P],
                           col[0:R, COL["gate_w2"]:COL["gate_w2"] + 1], start=True, stop=True)
                i.then_inc(s["gate_pre"], 1)

            def response(t):
                pe.wait_ge(s["oF_ready"], t + 1)
                if t == 0:
                    pe.wait_ge(s["gs_mc"], 4)
                    pe.wait_ge(s["x1_ready"], 2)
                else:
                    pe.wait_ge(s["r_ready"], 1)
                for c in range(Q):
                    sl = slice(c * P, (c + 1) * P)
                    i = mm(B0[:, sl], oF[t][:, sl], m3[:], start=True, stop=True)
                i.then_inc(s["resp_ready"], 1)

            def gs_matrix():
                pe.wait_ge(s["gs_uv"], 2)
                mm(G[:, 0:P], vo[:], uo[:], start=True, stop=True).then_inc(s["gs_m"], 1)
                pe.wait_ge(s["gs_mc"], 1)
                mm(G[0:R, 0:P], uo[:, 0:R], vo[:], start=True, stop=True).then_inc(s["gs_m"], 1)
                pe.wait_ge(s["gs_mc"], 2)
                mm(G[:, 0:P], basisR[:], respw[:], start=True, stop=True).then_inc(s["gs_m"], 1)
                pe.wait_ge(s["gs_mc"], 3)
                mm(G[:, 0:P], basisT[:], t2[:], start=True, stop=True).then_inc(s["gs_m"], 1)
                pe.wait_ge(s["gs_mc"], 4)

            L0_first(0)
            L0_second(0)
            L0_first(1)
            L0_third(0)
            L0_second(1)
            gs(2)
            L0_third(1)
            gs(2)
            to_F(n[0], [("n0_ready", 1)], "aF_pre")
            L1_down(0)
            gs(2)
            to_F(n[1], [("n0_ready", 2), ("aF_ready", 1)], "aF_pre")
            L1_down(1)
            gs(2)
            for t in range(NT):
                L1_expert(t)
                L1_up(t)
                gs(2)
            to_F(n[0], [("nq_ready", 1), ("aF_ready", 2)], "hF_pre")
            qkv(0)
            values(0)
            gs(2)
            to_F(n[1], [("nq_ready", 2), ("hF_ready", 1)], "hF_pre")
            qkv(1)
            gs(1)
            scores(0)
            gs(1)
            for r in range(Q):
                subtract(0, r)
            gs(1)
            values(1)
            gs(1)
            scores(1)
            gs(1)
            context(0)
            for r in range(Q):
                subtract(1, r)
            gs(1)
            to_F(cT[0], [("ctx_ready", 2), ("hF_ready", 2)], "cF_pre")
            wo(0)
            gs(1)
            context(1)
            gs(1)
            to_F(n[0], [("nf_ready", 1), ("cF_ready", 1)], "fF_pre")
            ff_in(0)
            gs(1)
            to_F(cT[1], [("ctx_ready", 4), ("fF_ready", 1)], "cF_pre")
            wo(1)
            gs(1)
            ff_out(0)
            gs(R)
            to_F(n[1], [("nf_ready", 2), ("cF_ready", 2)], "fF_pre")
            ff_in(1)
            gs_matrix()
            to_F(oT[0], [("o_ready", 1), ("fF_ready", 2)], "oF_pre")
            ff_out(1)
            gate(0)
            gate2(0)
            response(0)
            to_F(oT[1], [("o_ready", 2), ("oF_ready", 1)], "oF_pre")
            gate(1)
            gate2(1)
            response(1)

        @block.scalar
        def _(act):
            def c_(name, r0=0, r1=P):
                return col[r0:r1, COL[name]:COL[name] + 1]

            def gs_step(i):
                act.wait_ge(s["gs_q"], i + 1)
                nc.scalar.activation(gsq[:], G[0:2 * R, 0:P], ACT.Square,
                                     accum_out=gsn2[:, i:i + 1]).then_inc(s["gs_sq"], 1)

            gs = stepper(gs_step)

            def L0_gelu(t):
                for k, (name, dst) in enumerate((("pre_nr", hnr[t][:]), ("pre_tsr", htsr[t][:]),
                                                 ("pre_sr0", hsr[t][:, 0:HT]),
                                                 ("pre_sr1", hsr[t][:, HT:2 * HT]))):
                    act.wait_ge(s[name], t + 1)
                    nc.scalar.activation(dst, S_[k][:], ACT.Gelu,
                                         bias=c_(("b1_nr", "b1_tsr", "b1_sr0", "b1_sr1")[k]))\
                        .then_inc(s["h_ready"], 1)

            def z_gelu(t):
                act.wait_ge(s["pre_z"], t + 1)
                nc.scalar.activation(zsr[t][:], B0[:], ACT.Gelu, bias=c_("b2_sr"))\
                    .then_inc(s["z_ready"], 1)

            def evac_n(pre, ready, t, dst, gamma, beta):
                act.wait_ge(s[pre], t + 1)
                nc.scalar.activation(dst, B2[:], ACT.Identity, bias=c_(beta), scale=c_(gamma))\
                    .then_inc(s[ready], 1)

            def hid_gelu(t):
                act.wait_ge(s["hid_pre"], t + 1)
                nc.scalar.activation(hid[t][:], S_[t][:, 0:P], ACT.Gelu, bias=c_("down_b"))\
                    .then_inc(s["hid_ready"], 1)

            def qk(t):
                act.wait_ge(s["q_pre"], t + 1)
                nc.scalar.activation(q32[t][:], B0[:], ACT.Identity, bias=c_("bq"))\
                    .then_inc(s["q_ready"], 1)
                act.wait_ge(s["k_pre"], t + 1)
                nc.scalar.activation(k32[t][:], B1[:], ACT.Identity, bias=c_("bk"))\
                    .then_inc(s["k_ready"], 1)
                act.wait_ge(s["q_ready"], t + 1)
                nc.scalar.copy(qh[t][:], q32[t][:]).then_inc(s["qh_ready"], 1)
                act.wait_ge(s["k_ready"], t + 1)
                nc.scalar.copy(kh[t][:], k32[t][:]).then_inc(s["kh_ready"], 1)

            def exps(t):
                for r in range(Q):
                    act.wait_ge(s["s_sub"], 4 * t + r + 1)
                    nc.scalar.activation(ex[t][:, r * HT:(r + 1) * HT], S_[r][:], ACT.Exp,
                                         scale=float(DH) ** -0.5).then_inc(s["ex_ready"], 1)

            def evac_c(t):
                act.wait_ge(s["cF_pre"], t + 1)
                nc.scalar.activation(cF[t][:], B2[:], ACT.Identity, bias=c_("bv"))\
                    .then_inc(s["cF_ready"], 1)

            def ff_gelu(t):
                for k in range(FF):
                    act.wait_ge(s["ff_pre"], 4 * t + k + 1)
                    nc.scalar.activation(g[t][:, k * HT:(k + 1) * HT], S_[k][:], ACT.Gelu,
                                         bias=c_(f"f{k}")).then_inc(s["g_ready"], 1)

            def evac_o(t):
                act.wait_ge(s["oF_pre"], t + 1)
                nc.scalar.copy(oF[t][:], B2[:]).then_inc(s["oF_ready"], 1)

            def gate_act(t):
                act.wait_ge(s["h1_pre"], t + 1)
                nc.scalar.activation(view(h1[t], 0, [(S, HB), (1, S)], rows=R),
                                     view(G, 0, [(1, HB), (0, S)], rows=R), ACT.Relu, bias=c_("gate_b1", 0, R),
                                     scale=1.0 / S).then_inc(s["h1_ready"], 1)
                act.wait_ge(s["gate_pre"], t + 1)
                if t == 0:
                    act.wait_ge(s["gb_ready"], 1)
                nc.scalar.activation(sact[:, t * Q:(t + 1) * Q], G[:, 0:Q], ACT.Tanh,
                                     bias=gb2h[:], scale=0.5).then_inc(s["gate_act"], 1)

            act.wait_ge(ld["small"], 112)
            nc.scalar.activation(smod[:], col[:, COL["safety0"]:COL["safety0"] + 8], ACT.Tanh,
                                 scale=0.5).then_inc(s["mod_ready"], 1)
            L0_gelu(0)
            z_gelu(0)
            L0_gelu(1)
            z_gelu(1)
            gs(4)
            for t in range(NT):
                evac_n("aF_pre", "aF_ready", t, aF[t][:], "gamma0", "beta0")
                hid_gelu(t)
                gs(2)
            gs(4)
            evac_n("hF_pre", "hF_ready", 0, hF[0][:], "gamma2a", "beta2a")
            qk(0)
            gs(2)
            evac_n("hF_pre", "hF_ready", 1, hF[1][:], "gamma2a", "beta2a")
            qk(1)
            gs(2)
            exps(0)
            gs(3)
            exps(1)
            gs(1)
            evac_c(0)
            gs(2)
            evac_n("fF_pre", "fF_ready", 0, fF[0][:], "gamma2", "beta2")
            ff_gelu(0)
            gs(1)
            evac_c(1)
            gs(1)
            gs(R)
            evac_n("fF_pre", "fF_ready", 1, fF[1][:], "gamma2", "beta2")
            ff_gelu(1)
            evac_o(0)
            gate_act(0)
            evac_o(1)
            gate_act(1)

        @block.gpsimd
        def _(pool):
            def gs_step(i):
                pool.wait_ge(s["gs_sq"], i + 1)
                nc.gpsimd.tensor_tensor(gsn[:, i:i + 1], gsn2[:, i:i + 1], half_pos[:], ALU.pow)\
                    .then_inc(s["gs_n"], 1)
                pool.wait_ge(s["gs_n"], i + 1)
                nc.gpsimd.tensor_scalar(gsne[:, i:i + 1], gsn[:, i:i + 1], GS_EPS, None, ALU.add)\
                    .then_inc(s["gs_ne"], 1)

            gs = stepper(gs_step)

            def rstd_(k, t):
                pool.wait_ge(s["mv_ready"], k)
                v = ve[:, t * Q:(t + 1) * Q]
                nc.gpsimd.tensor_scalar(v, view(mv, t * Q * 2 + 1, [(2, Q)]), EPS, None, ALU.add)\
                    .then_inc(s["ve_ready"], 1)
                pool.wait_ge(s["ve_ready"], k)
                nc.gpsimd.tensor_tensor(rstd[:, t * Q:(t + 1) * Q], v, half_neg[:, 0:Q], ALU.pow)\
                    .then_inc(s["rstd_ready"], 1)

            def bc(t_, i=0):
                return view(t_, i * P, [(0, Q), (1, P)])

            def q4(t_):
                return view(t_, 0, [(P, Q), (1, P)])

            def a0(t):
                pool.wait_ge(s["n0_ready"], t + 1)
                nc.gpsimd.tensor_tensor(q4(tmp[t]), q4(n[t]), bc(rows, ROW["gamma0"]), ALU.mult)\
                    .then_inc(s["a0_tmp"], 1)
                pool.wait_ge(s["a0_tmp"], t + 1)
                nc.gpsimd.tensor_tensor(q4(a0T[t]), q4(tmp[t]), bc(b0u), ALU.add)\
                    .then_inc(s["a0T_ready"], 1)

            def a1(t):
                pool.wait_ge(s["a1_ready"], t + 1)
                nc.gpsimd.tensor_tensor(q4(a1bo[t]), q4(a1T[t]), bc(rows, ROW["bo"]), ALU.add)\
                    .then_inc(s["a1bo_ready"], 1)

            def xd_(t):
                pool.wait_ge(s["x1_ready"], t + 1)
                nc.gpsimd.tensor_tensor(xd[t][:], x1[t][:], a1T[t][:], ALU.subtract)\
                    .then_inc(s["xd_tmp"], 1)
                pool.wait_ge(s["xd_tmp"], t + 1)
                nc.gpsimd.tensor_tensor(q4(xd[t]), q4(xd[t]), bc(rows, ROW["b2"]), ALU.add)\
                    .then_inc(s["xd_ready"], 1)

            pool.wait_ge(ld["small"], 112)
            nc.gpsimd.memset(expbd[:], 0.0).then_inc(s["zeroed"], 1)
            nc.gpsimd.memset(half_neg[:], -0.5).then_inc(s["halves_ready"], 1)
            nc.gpsimd.memset(half_pos[:], 0.5).then_inc(s["halves_ready"], 1)
            for t in range(NT):
                nc.gpsimd.memset(vbd[t][:], 0.0)\
                    .then_inc(s["zeroed"], 1)
                pool.wait_ge(s["zeroed"], 2 + t)
                nc.gpsimd.tensor_copy(view(vbd[t], A, [(HD, HB * Q), (1, Q)]),
                                      view(keymask, 0, [(0, HB * Q), (1, Q)]))\
                    .then_inc(s["vones_ready"], 1)
            pool.wait_ge(ld["small"], 112)
            nc.gpsimd.tensor_scalar(gb2h[:], col[:, COL["gate_b2"]:COL["gate_b2"] + 1], 0.5, None,
                                    ALU.mult).then_inc(s["gb_ready"], 1)
            pool.wait_ge(ld["rows"], 16)
            nc.gpsimd.tensor_tensor(b0u[:], rows[:, ROW["beta0"] * P:(ROW["beta0"] + 1) * P],
                                    rows[:, ROW["up_b"] * P:(ROW["up_b"] + 1) * P], ALU.add)\
                .then_inc(s["rowsums_ready"], 1)
            nc.gpsimd.tensor_tensor(rsb[:], rows[:, ROW["resp_b"] * P:(ROW["resp_b"] + 1) * P],
                                    rows[:, ROW["safety_bias"] * P:(ROW["safety_bias"] + 1) * P],
                                    ALU.add).then_inc(s["rowsums_ready"], 1)
            pool.wait_ge(s["halves_ready"], 2)
            pool.wait_ge(s["rowsums_ready"], 2)
            rstd_(1, 0)
            gs(2)
            rstd_(2, 1)
            gs(2)
            for t in range(NT):
                a0(t)
                gs(2)
            rstd_(3, 0)
            gs(2)
            rstd_(4, 1)
            gs(2)
            rstd_(5, 0)
            rstd_(6, 1)
            a1(0)
            a1(1)
            gs(8)
            rstd_(7, 0)
            xd_(0)
            gs(3)
            rstd_(8, 1)
            xd_(1)
            gs(R)

        @block.vector
        def _(dve):
            v = nc.vector

            def gs_step(i):
                dve.wait_ge(s["gs_sq"], i + 1)
                if i == 0:
                    dve.wait_ge(ld["gs"], 64)
                v.tensor_tensor_reduce(gsjunk[:], uv[:], G[0:2 * R, 0:P], gsneg[:, i:i + 1], 0.0,
                                       ALU.mult, ALU.add, gsc[:, i:i + 1]).then_inc(s["gs_c"], 1)
                dve.wait_ge(s["gs_ne"], i + 1)
                v.reciprocal(gsr[:, i:i + 1], gsne[:, i:i + 1]).then_inc(s["gs_rec"], 1)
                dve.wait_ge(s["gs_c"], i + 1)
                dve.wait_ge(s["gs_rec"], i + 1)
                v.tensor_scalar(gsf[:, i:i + 1], gsc[:, i:i + 1], gsr[:, i:i + 1],
                                gsr[:, i:i + 1], ALU.mult, ALU.mult).then_inc(s["gs_f"], 1)
                dve.wait_ge(s["gs_f"], i + 1)
                v.scalar_tensor_tensor(uv[:], G[0:2 * R, 0:P], gsf[:, i:i + 1], uv[:],
                                       ALU.mult, ALU.add).then_inc(s["gs_col"], 1)

            gs = stepper(gs_step)

            def norm(k, t, source):
                for c in range(Q):
                    v.bn_stats(st[:, (t * Q + c) * 6:(t * Q + c + 1) * 6],
                               source[:, c * P:(c + 1) * P]).then_inc(s["stats"], 1)
                for c in range(Q):
                    dve.wait_ge(s["stats"], 4 * (k - 1) + c + 1)
                    i = v.bn_aggr(mv[:, (t * Q + c) * 2:(t * Q + c + 1) * 2],
                                  st[:, (t * Q + c) * 6:(t * Q + c + 1) * 6])
                i.then_inc(s["mv_ready"], 1)

            def apply(k, t, source, signal):
                dve.wait_ge(s["rstd_ready"], k)
                dve.wait_ge(s["mv_ready"], k)
                for c in range(Q):
                    m = (t * Q + c) * 2
                    i = v.tensor_scalar(n[t][:, c * P:(c + 1) * P], source[:, c * P:(c + 1) * P],
                                        mv[:, m:m + 1], rstd[:, t * Q + c:t * Q + c + 1],
                                        ALU.subtract, ALU.mult)
                i.then_inc(s[signal], 1)

            def bc(t_, i=0):
                return view(t_, i * P, [(0, Q), (1, P)])

            def q4(t_):
                return view(t_, 0, [(P, Q), (1, P)])

            dve.wait_ge(ld["small"], 112)
            v.tensor_copy(condf[:], cond_i[:]).then_inc(s["ids_step"], 1)
            v.tensor_scalar(ids[:], ids_i[:], -1.0, float(E), ALU.max, ALU.min)\
                .then_inc(s["ids_step"], 1)
            dve.wait_ge(s["ids_step"], 2)
            v.tensor_scalar(view(chosen, 0, [(S, B), (1, S)], rows=3),
                            view(condf, 0, [(1, B), (0, S)], rows=3), cidx[:], None, ALU.is_equal)\
                .then_inc(s["chosen_ready"], 1)
            v.tensor_scalar(other[:], condf[:], cidx[:], None, ALU.not_equal)\
                .then_inc(s["chosen_ready"], 1)
            v.tensor_scalar(onehot[:], ids[:], col[0:EX, COL["expert_id"]:COL["expert_id"] + 1],
                            None, ALU.is_equal).then_inc(s["onehot_ready"], 1)
            dve.wait_ge(s["expert_picked"], 1)
            dve.wait_ge(s["zeroed"], 1)
            for c in range(Q):
                for o4 in range(Q):
                    i = v.tensor_copy(
                        view(expbd, c * A + o4, [(Q * P, NT), (P, Q), (Q, A // Q)], c * A, A),
                        view(G, c * Q, [(HB, NT), (1, Q), (B, A // Q)], o4 * A, A))
                i.then_inc(s["expbd_ready"], 1)
            for c in range(Q):
                i = v.tensor_copy(view(expb, 0, [(Q, NT), (1, Q)], c * A, A),
                                  view(G, 256 + c * Q, [(HB, NT), (1, Q)], c * A, A))
            i.then_inc(s["expbd_ready"], 1)

            def sum0(t):
                dve.wait_ge(s["y0_ready"], t + 1)
                if t == 0:
                    dve.wait_ge(ld["xT"], 32)
                v.tensor_tensor(y[t][:], B1[:], xT[:, t * HT:(t + 1) * HT], ALU.add)\
                    .then_inc(s["y0_sum"], 1)
                dve.wait_ge(s["y0_sum"], t + 1)

            def hidden2(t):
                dve.wait_ge(s["hid2_pre"], t + 1)
                dve.wait_ge(s["expbd_ready"], 5)
                v.tensor_tensor(view(hid2[t], 0, [(S, Q), (1, S)]),
                                view(S_[2 + t], 0, [(S, Q), (1, S)]),
                                view(expb, t * Q, [(1, Q), (0, S)]), ALU.add)\
                    .then_inc(s["hid2_ready"], 1)

            def sum1(t):
                dve.wait_ge(s["up_ready"], t + 1)
                dve.wait_ge(s["a0T_ready"], t + 1)
                v.tensor_tensor(y[t][:], B1[:], a0T[t][:], ALU.add).then_inc(s["y1_sum"], 1)
                dve.wait_ge(s["y1_sum"], t + 1)

            def affine1(t):
                dve.wait_ge(s["n1_ready"], t + 1)
                v.tensor_tensor(q4(tmp[t]), q4(n[t]), bc(rows, ROW["gamma1"]), ALU.mult)\
                    .then_inc(s["a1_tmp"], 1)
                dve.wait_ge(s["a1_tmp"], t + 1)
                v.tensor_tensor(q4(a1T[t]), q4(tmp[t]), bc(rows, ROW["beta1"]), ALU.add)\
                    .then_inc(s["a1_ready"], 1)
                dve.wait_ge(s["a1_ready"], t + 1)

            def qs_(t_):
                return view(t_, 0, [(S, HB), (1, S)])

            def split(t):
                dve.wait_ge(s["kh_ready"], t + 1)
                v.tensor_tensor(ql[t][:], q32[t][:], qh[t][:], ALU.subtract)\
                    .then_inc(s["ql_ready"], 1)
                v.tensor_tensor(kl[t][:], k32[t][:], kh[t][:], ALU.subtract)
                for h in range(Q):
                    v.tensor_scalar(view(qbh[t], h * S, [(P, HB), (1, S)]), qs_(qh[t]),
                                    headmask[:, h:h + 1], None, ALU.mult)
                dve.wait_ge(s["ql_ready"], t + 1)
                for h in range(Q):
                    i = v.tensor_scalar(view(qbl[t], h * S, [(P, HB), (1, S)]), qs_(ql[t]),
                                        headmask[:, h:h + 1], None, ALU.mult)
                i.then_inc(s["qk_split"], 1)

            def values(t):
                if t == 0:
                    dve.wait_ge(s["vones_ready"], 2)
                dve.wait_ge(s["v_pre"], t + 1)
                for h in range(Q):
                    v.tensor_copy(view(vbd[t], h * DH, [(HD, HB * Q), (1, DH)], h * S, S),
                                  view(S_[t], 0, [(DH, HB * Q), (1, DH)], h * S, S))\
                        .then_inc(s["v_ready"], 1)

            def maxima(t):
                for r in range(Q):
                    dve.wait_ge(s["s_ready"], 4 * t + r + 1)
                    v.tensor_reduce(mx[t][:, r * HB:(r + 1) * HB],
                                    view(S_[r], 0, [(S, HB), (1, S)]), AX.X, ALU.max,
                                    negate=True).then_inc(s["mx_ready"], 1)

            def turn(t):
                for r in range(Q):
                    sl = slice(r * HT, (r + 1) * HT)
                    dve.wait_ge(s["ex_ready"], 4 * t + r + 1)
                    v.transpose(exT[t][:, sl], ex[t][:, sl]).then_inc(s["exT_ready"], 1)

            def softmax_end(t):
                dve.wait_ge(s["pv_ready"], t + 1)
                for k, bank in enumerate((B0, B1)):
                    rd = view(rden[t], k * 2 * NH, [(Q, 2 * Q), (1, Q)])
                    v.reciprocal(rd, view(bank, A, [(HD, 2 * Q), (1, Q)]))\
                        .then_inc(s["rden_ready"], 1)
                    dve.wait_ge(s["rden_ready"], 2 * t + k + 1)
                    v.tensor_tensor(view(cT[t], k * 2 * P, [(A, 2 * Q), (DH, Q), (1, DH)]),
                                    view(bank, 0, [(HD, 2 * Q), (DH, Q), (1, DH)]),
                                    view(rden[t], k * 2 * NH, [(Q, 2 * Q), (1, Q), (0, DH)]),
                                    ALU.mult).then_inc(s["ctx_ready"], 1)

            def sum_x1(t):
                dve.wait_ge(s["wo_ready"], t + 1)
                dve.wait_ge(s["a1bo_ready"], t + 1)
                v.tensor_tensor(x1[t][:], B0[:], a1bo[t][:], ALU.add).then_inc(s["x1_ready"], 1)
                dve.wait_ge(s["x1_ready"], t + 1)

            def gated(t):
                dve.wait_ge(s["ff_ready"], t + 1)
                dve.wait_ge(s["xd_ready"], t + 1)
                v.tensor_tensor(tmp[t][:], B1[:], xd[t][:], ALU.add).then_inc(s["u_ready"], 1)
                dve.wait_ge(s["u_ready"], t + 1)
                for c in range(Q):
                    sl = slice(c * P, (c + 1) * P)
                    k = COL["gate0"] + t * Q + c
                    i = v.scalar_tensor_tensor(oT[t][:, sl], tmp[t][:, sl], col[:, k:k + 1],
                                               a1T[t][:, sl], ALU.mult, ALU.add)
                i.then_inc(s["o_ready"], 1)

            def pooled(t):
                dve.wait_ge(s["oF_ready"], t + 1)
                v.tensor_reduce(pool_s[t][:], view(oF[t], 0, [(S, HB), (1, S)]), AX.X, ALU.add)\
                    .then_inc(s["pooled"], 1)

            def strength(t):
                dve.wait_ge(s["gate_act"], t + 1)
                sl = slice(t * Q, (t + 1) * Q)
                v.scalar_tensor_tensor(stren[:, sl], sact[:, sl], 1.0, smod4[:, sl], ALU.add,
                                       ALU.mult).then_inc(s["stren_ready"], 1)

            def final(t):
                dve.wait_ge(s["resp_ready"], t + 1)
                v.tensor_tensor(q4(tmp[t]), q4(B0), bc(rsb), ALU.add).then_inc(s["r_ready"], 1)
                dve.wait_ge(s["r_ready"], t + 1)
                strength(t)
                dve.wait_ge(s["stren_ready"], t + 1)
                for c in range(Q):
                    sl = slice(c * P, (c + 1) * P)
                    k = t * Q + c
                    i = v.scalar_tensor_tensor(res[t][:, sl], tmp[t][:, sl], stren[:, k:k + 1],
                                               oT[t][:, sl], ALU.mult, ALU.add)
                i.then_inc(s["res_ready"], 1)

            def gs_finish():
                v.tensor_tensor_reduce(gsjunk[:, 0:R], gsr[:], gsdiag[:], 1.0, 0.0, ALU.mult,
                                       ALU.add, gsd[:, 0:1]).then_inc(s["gs_d"], 1)
                dve.wait_ge(s["gs_d"], 1)
                dve.wait_ge(s["gs_col"], R)
                for k, dst in enumerate((uo, vo)):
                    v.tensor_scalar(dst[:], uv[k * R:(k + 1) * R, :], gsd[k * R:(k + 1) * R, 0:1],
                                    None, ALU.mult).then_inc(s["gs_uv"], 1)
                for k, (dst, n_) in enumerate(((basisT, P), (basisR, R), (t2, P), (m3, P))):
                    dve.wait_ge(s["gs_m"], k + 1)
                    v.tensor_copy(dst[:], G[0:n_, 0:P]).then_inc(s["gs_mc"], 1)

            dve.wait_ge(s["mod_ready"], 1)
            v.tensor_scalar(smod4[:], smod[:], 0.25, 0.25, ALU.mult, ALU.add)\
                .then_inc(s["stren_step"], 1)
            dve.wait_ge(s["stren_step"], 1)
            sum0(0)
            norm(1, 0, y[0])
            apply(1, 0, y[0], "n0_ready")
            gs(2)
            sum0(1)
            norm(2, 1, y[1])
            apply(2, 1, y[1], "n0_ready")
            gs(2)
            gs(4)
            for t in range(NT):
                hidden2(t)
                sum1(t)
                norm(3 + t, t, y[t])
                gs(2)
            dve.wait_ge(ld["rows"], 16)
            for t in range(NT):
                apply(3 + t, t, y[t], "n1_ready")
                affine1(t)
                norm(5 + t, t, a1T[t])
                apply(5 + t, t, a1T[t], "nq_ready")
            dve.wait_ge(ld["w2"], 80)
            split(0)
            values(0)
            gs(2)
            split(1)
            gs(1)
            maxima(0)
            gs(1)
            turn(0)
            gs(1)
            values(1)
            gs(1)
            maxima(1)
            gs(1)
            softmax_end(0)
            turn(1)
            gs(1)
            sum_x1(0)
            norm(7, 0, x1[0])
            apply(7, 0, x1[0], "nf_ready")
            gs(1)
            softmax_end(1)
            gs(1)
            gs(1)
            sum_x1(1)
            norm(8, 1, x1[1])
            apply(8, 1, x1[1], "nf_ready")
            gs(1)
            gs(R)
            gs_finish()
            gated(0)
            gated(1)
            pooled(0)
            final(0)
            pooled(1)
            final(1)


_OUT = "out_0_dram"


def layout(i):
    f = {k.replace("_cond_", "_"): np.asarray(v) for k, v in i.items()}
    c = np.ascontiguousarray
    x = f["x"].reshape(8, P, P)
    xF = x.reshape(8 * P, P).T
    xT = x.transpose(1, 0, 2).reshape(P, 8 * P)
    out = {}
    out["xFa"], out["xFb"] = c(xF[:, :HT]), c(xF[:, HT:])
    out["xTa"], out["xTb"] = c(xT[:, :HT]), c(xT[:, HT:])
    out["w0a"] = c(np.concatenate([f["L0_w1_nr"], f["L0_w1_tsr"], f["L0_w1_sr"]], 1))
    out["w0b"] = c(np.concatenate([f["L0_w2_nr"], f["L0_w2_tsr"], f["L0_w2_sr"][:P],
                                   f["L0_w2_sr"][P:], f["L0_w3_sr"]], 1))
    up = np.zeros((Q, A, Q, P), np.float32)
    for q in range(Q):
        up[q, :, q] = f["L1_up_W"].T
    out["w1"] = c(np.concatenate([f["L1_down_W"].T, up.reshape(P, Q * P), f["L3_gate_w1"].T], 1))
    out["w2"] = c(np.concatenate([f[f"L2_W{k}"] for k in "qkvo"], 1))
    w2 = f["L2_W2"].reshape(FF, P, P).transpose(1, 0, 2).reshape(P, FF * P)
    out["w3"] = c(np.concatenate([f["L2_W1"], w2], 1))

    def tokens(a):
        return np.repeat(a.reshape(8, Q), S, axis=1).T

    def padded(a, fill=0.0):
        return np.concatenate([a, np.full(P - len(a), fill, np.float32)])

    cols = {"b1_nr": f["L0_b1_nr"], "b1_tsr": f["L0_b1_tsr"], "b1_sr0": f["L0_b1_sr"][:P],
            "b1_sr1": f["L0_b1_sr"][P:], "b2_sr": f["L0_b2_sr"], "gamma0": f["L0_gamma"],
            "beta0": f["L0_beta"], "down_b": np.tile(f["L1_down_b"], Q),
            "gamma2a": f["L2_gamma1"], "beta2a": f["L2_beta1"], "bq": f["L2_bq"],
            "bk": f["L2_bk"], "bv": f["L2_bv"], "gamma2": f["L2_gamma2"], "beta2": f["L2_beta2"],
            "gate_b1": padded(f["L3_gate_b1"]), "gate_w2": padded(f["L3_gate_w2"][0]),
            "gate_b2": np.repeat(f["L3_gate_b2"], P),
            "expert_id": padded(np.array([*range(E), E, -1], np.float32))}
    cols |= {f"f{k}": f["L2_b1"][k * P:(k + 1) * P] for k in range(FF)}
    cols |= {f"gate{k}": tokens(f["condB_gatescore"])[:, k] for k in range(8)}
    cols |= {f"safety{k}": tokens(f["condB_safetyscore"])[:, k] for k in range(8)}
    out["col"] = c(np.stack([cols[k] for k in COLS], 1))
    rows = {"gamma0": "L0_gamma", "beta0": "L0_beta", "up_b": "L1_up_b", "gamma1": "L1_ln_gamma",
            "beta1": "L1_ln_beta", "bo": "L2_bo", "b2": "L2_b2", "resp_b": "L3_resp_b",
            "safety_bias": "L3_safety_bias"}
    out["rows"] = c(np.broadcast_to(np.concatenate([f[rows[k]] for k in ROWS]), (P, len(ROWS) * P)))
    out["uv"] = c(np.concatenate([f["L3_U"].T, f["L3_V"].T], 0))
    out["respw"] = c(f["L3_resp_w"].T)
    eye = np.eye(A, dtype=np.float32).reshape(1, A * A)
    out["expw"] = c(np.concatenate([f["L1_expert_W"].reshape(E, A * A), eye, eye], 0))
    none = np.zeros((2, A), np.float32)
    emb = f["L1_domain_emb"]
    out["expbe"] = c(np.concatenate([np.tile(np.concatenate([f["L1_expert_b"], none], 0), Q),
                                     np.tile(np.concatenate([emb, emb[-1:], emb[:1]], 0), Q)], 1))
    out["ids"] = c(np.broadcast_to(f["itok_B_0_15"], (EX, B)))
    out["cond"] = c(np.broadcast_to(f["itok_B_0_2"], (3, B)))
    out["b2c"] = c(np.stack([f["L0_b2_nr"], f["L0_b2_tsr"], f["L0_b3_sr"]], 0))
    p = np.arange(P)
    out["ident"] = np.eye(P, dtype=np.float32)
    p64 = np.arange(2 * R)[:, None] % R
    out["gsneg"] = c(-(p64 > np.arange(R)[None]).astype(np.float32))
    out["gsdiag"] = c((p64 == np.arange(R)[None]).astype(np.float32))
    out["headmask"] = c(((p[:, None] % A) // DH == np.arange(Q)[None]).astype(np.float32))
    out["keymask"] = c((p[:, None] // A == np.arange(Q)[None]).astype(np.float32))
    out["cidx"] = np.arange(3, dtype=np.float32)[:, None]
    bf = np.dtype("bfloat16")
    out["identb"] = np.eye(P).astype(bf)
    out["maskl"] = c((p[:, None] % S == p[None] % S).astype(bf))
    out["maskr"] = c(np.where(np.arange(S)[None] > p[:, None] % S, MASKED, 0.0).astype(bf))
    out["offb"] = (np.eye(3) * OFF).astype(bf)
    return out


def kernel(**inputs):
    import concourse.bacc as bacc
    from concourse.bass_utils import run_bass_kernel_spmd

    nc = bacc.Bacc("TRN2", target_bir_lowering=False, num_devices=1)
    arrays = layout(inputs)
    src = {k: nc.dram_tensor("in_" + k, a.shape, mybir.dt.from_np(a.dtype), kind="ExternalInput").ap()
           for k, a in arrays.items()}
    out = nc.dram_tensor(_OUT, (P, 8 * P), F32, kind="ExternalOutput").ap()
    build(nc, src, out)
    r = run_bass_kernel_spmd(nc, [{"in_" + k: a for k, a in arrays.items()}], core_ids=[0])
    got = r.results[0][_OUT].reshape(P, 8, P)
    return np.ascontiguousarray(got.transpose(1, 0, 2)).reshape(B, S, P)
```

```python
from contextlib import ExitStack

import numpy as np
import concourse.bass as bass
from concourse import mybir

F32 = mybir.dt.float32
BF16 = mybir.dt.bfloat16
F16 = mybir.dt.float16
I32 = mybir.dt.int32
ALU = mybir.AluOpType
ACT = mybir.ActivationFunctionType
AX = mybir.AxisListType

P = 128
S = 32
B = 32
NH = 16
DH = P // NH
A = 32
E = 16
EX = E + 2
R = 32
Q = 4
NT = 2
HT = B * S // NT
HB = B // NT
FF = 4
HD = A + Q
EPS = 1e-5
GS_EPS = 1e-8
OFF = -1e9
MASKED = -1e30
L0_ORDER = (2, 3, 0, 1)

COLS = ["b1_nr", "b1_tsr", "b1_sr0", "b1_sr1", "b2_sr", "gamma0", "beta0", "down_b",
        "gamma2a", "beta2a", "bq", "bk", "bv", "gamma2", "beta2", "f0", "f1", "f2", "f3",
        "gate_b1", "gate_w2", "gate_b2", "expert_id"] + \
       [f"gate{c}" for c in range(8)] + [f"safety{c}" for c in range(8)] + \
       [f"head{h}" for h in range(Q)] + [f"quad{h}" for h in range(Q)] + ["branch"]
COL = {n: i for i, n in enumerate(COLS)}
ROWS = ["gamma0", "beta0", "up_b", "gamma1", "beta1", "bo", "b2", "resp_b", "safety_bias"]
ROW = {n: i for i, n in enumerate(ROWS)}


def build(nc, src, out_dram):
    with ExitStack() as ctx:
        def sb(name, cols, dt=F32, rows=P):
            return ctx.enter_context(nc.sbuf_tensor(name, [rows, cols], dt))

        def sem(name):
            return ctx.enter_context(nc.semaphore(name))

        def view(t, off, dims, p0=0, rows=P):
            a = t[p0:p0 + rows, off:off + 1]
            return bass.AP(a.tensor, a.offset, [list(a.ap[0])] + [list(d) for d in dims])

        xF = sb("xF", NT * HT)
        xT = sb("xT", NT * HT)
        w0 = sb("w0", 9 * P)
        col = sb("col", len(COLS))
        rows = sb("rows", len(ROWS) * P)
        w1 = sb("w1", A + Q * P + A)
        w2 = sb("w2", 4 * P)
        w3 = sb("w3", 2 * FF * P)
        gs_pack = sb("gs_pack", 2 * P + 2 * R)
        exp_pack = sb("exp_pack", A * A + 4 * P, rows=R)
        bf_pack = sb("bf_pack", 2 * P + S + 3, BF16)
        id_pack = sb("id_pack", 2 * B, I32, rows=EX)

        ident = gs_pack[:, 0:P]
        uv = gs_pack[0:2 * R, P:2 * P]
        gsneg = gs_pack[0:2 * R, 2 * P:2 * P + R]
        gsdiag = gs_pack[0:2 * R, 2 * P + R:2 * P + 2 * R]
        expw = exp_pack[0:EX, 0:A * A]
        expbe = exp_pack[0:EX, A * A:A * A + 2 * P]
        b2c = exp_pack[0:3, A * A + 2 * P:A * A + 3 * P]
        respw = exp_pack[:, A * A + 3 * P:A * A + 4 * P]
        identb = bf_pack[:, 0:P]
        maskl = bf_pack[:, P:2 * P]
        maskr = bf_pack[:, 2 * P:2 * P + S]
        offb = bf_pack[0:3, 2 * P + S:]
        ids_i = id_pack[:, 0:B]
        cond_i = id_pack[0:3, B:2 * B]
        headmask = col[:, COL["head0"]:COL["head0"] + Q]
        keymask = col[:, COL["quad0"]:COL["quad0"] + Q]
        cidx = col[0:3, COL["branch"]:COL["branch"] + 1]

        ids = sb("ids", B, rows=EX)
        onehot = sb("onehot", B, rows=EX)
        condf = sb("condf", B, rows=3)
        chosen = sb("chosen", B * S, rows=3)
        other = sb("other", B, BF16, rows=3)
        half_neg = sb("half_neg", 8)
        half_pos = sb("half_pos", 1, rows=2 * R)
        expbd = sb("expbd", NT * Q * P)
        expb = sb("expb", NT * Q)
        b0u = sb("b0u", P)
        rsb = sb("rsb", P)
        hnr = [sb(f"hnr{t}", HT) for t in range(NT)]
        htsr = [sb(f"htsr{t}", HT) for t in range(NT)]
        hsr = [sb(f"hsr{t}", 2 * HT) for t in range(NT)]
        zsr = [sb(f"zsr{t}", HT) for t in range(NT)]
        y = [sb(f"y{t}", HT) for t in range(NT)]
        n = [sb(f"n{t}", HT) for t in range(NT)]
        st = sb("st", NT * Q * 6)
        mv = sb("mv", NT * Q * 2)
        ve = sb("ve", NT * Q)
        rstd = sb("rstd", NT * Q)
        aF = [sb(f"aF{t}", HT) for t in range(NT)]
        a0T = [sb(f"a0T{t}", HT) for t in range(NT)]
        tmp = [sb(f"tmp{t}", HT) for t in range(NT)]
        hid = [sb(f"hid{t}", P) for t in range(NT)]
        hid2 = [sb(f"hid2{t}", P) for t in range(NT)]
        a1T = [sb(f"a1T{t}", HT) for t in range(NT)]
        hF = [sb(f"hF{t}", HT) for t in range(NT)]
        q32, k32 = hnr, htsr
        qh = [sb(f"qh{t}", HT, F16) for t in range(NT)]
        ql = [sb(f"ql{t}", HT, F16) for t in range(NT)]
        kh = [sb(f"kh{t}", HT, F16) for t in range(NT)]
        kl = [sb(f"kl{t}", HT, F16) for t in range(NT)]
        qbh = [sb(f"qbh{t}", Q * HT, F16) for t in range(NT)]
        qbl = [sb(f"qbl{t}", Q * HT, F16) for t in range(NT)]
        vbd = [sb(f"vbd{t}", HB * Q * HD) for t in range(NT)]
        mx = [sb(f"mx{t}", Q * HB, BF16) for t in range(NT)]
        ex = [sb(f"ex{t}", Q * HT) for t in range(NT)]
        exT = [sb(f"exT{t}", Q * HT) for t in range(NT)]
        rden = [sb(f"rden{t}", Q * NH) for t in range(NT)]
        cT = [sb(f"cT{t}", HT) for t in range(NT)]
        cF = [sb(f"cF{t}", HT) for t in range(NT)]
        x1 = [sb(f"x1{t}", HT) for t in range(NT)]
        a1bo = [sb(f"a1bo{t}", HT) for t in range(NT)]
        xd = [sb(f"xd{t}", HT) for t in range(NT)]
        fF = hF
        g = ex
        oT = [sb(f"oT{t}", HT) for t in range(NT)]
        oF = cF
        pool_s = [sb(f"pool{t}", HB) for t in range(NT)]
        h1 = [sb(f"h1{t}", HT, rows=R) for t in range(NT)]
        gb2h = sb("gb2h", 1)
        sact = sb("sact", 8)
        smod = sb("smod", 8)
        smod4 = sb("smod4", 8)
        stren = sb("stren", 8)
        res = y
        gsq = sb("gsq", P, rows=2 * R)
        gsjunk = sb("gsjunk", P, rows=2 * R)
        gsn2 = sb("gsn2", R, rows=2 * R)
        gsn = sb("gsn", R, rows=2 * R)
        gsne = sb("gsne", R, rows=2 * R)
        gsr = sb("gsr", R, rows=2 * R)
        gsr2 = sb("gsr2", R, rows=2 * R)
        minus_two = sb("minus_two", 1, rows=2 * R)
        gsc = sb("gsc", R, rows=2 * R)
        gsf = sb("gsf", R, rows=2 * R)
        gsd = sb("gsd", R + 1, rows=2 * R)
        uo = sb("uo", P, rows=R)
        vo = sb("vo", P, rows=R)
        basisT = sb("basisT", P)
        basisR = sb("basisR", P, rows=R)
        t2 = sb("t2", P)
        m3 = sb("m3", P)
        filler = sb("filler", HT, BF16)

        S_ = [ctx.enter_context(nc.psum_tensor(f"S{i}", [P, 512], F32)) for i in range(4)]
        B0 = ctx.enter_context(nc.psum_tensor("B0", [P, 512], F32))
        B1 = ctx.enter_context(nc.psum_tensor("B1", [P, 512], F32))
        B2 = ctx.enter_context(nc.psum_tensor("B2", [P, 512], F32))
        G = ctx.enter_context(nc.psum_tensor("G", [P, 512], F32))

        ld = {k: sem("ld_" + k) for k in ("ids", "col", "bf", "w0", "x0", "w0b", "gs", "expert",
                                          "x1", "xT", "w1", "rows", "w2", "w3")}
        s = {k: sem(k) for k in (
            "filler_ready",
            "onehot_ready", "chosen_ready", "expert_picked", "expbd_ready",
            "zeroed", "halves_ready", "rowsums_ready", "vones_ready", "ids_step",
            "pre_ready", "h_ready", "pre_z", "z_ready", "y0_ready",
            "y0_sum", "y1_sum", "x1_ready", "a0_tmp", "a0T_ready",
            "aF_pre", "aF_ready", "hF_pre", "hF_ready", "fF_pre", "fF_ready",
            "hid_pre", "hid_ready", "hid2_pre", "hid2_ready", "up_ready", "a1_tmp", "a1_ready",
            "q_pre", "k_pre", "q_ready", "k_ready", "qh_ready", "kh_ready", "ql_ready", "q_split", "k_split",
            "v_pre", "v_ready", "s_ready", "mx_ready", "s_sub", "ex_ready", "exT_ready",
            "pv_ready", "rden_ready", "ctx_ready", "cF_pre", "cF_ready", "wo_ready",
            "a1bo_ready", "xd_tmp", "xd_ready",
            "ff_pre", "g_ready", "ff_ready", "u_ready", "o_ready", "oF_pre", "oF_ready",
            "pool_pre", "pooled", "h1_pre", "h1_ready", "gate_pre", "gate_act", "mod_ready", "stren_step",
            "stren_ready", "resp_ready", "r_ready", "res_ready", "stored", "gb_ready",
            "gs_q", "gs_sq", "gs_n", "gs_ne", "gs_c", "gs_rec", "gs_f", "gs_col",
            "gs_d", "gs_uv", "gs_m", "gs_mc",
        )}
        ln = [{k: sem(f"ln{i}_{k}") for k in ("stats", "mv", "ve", "rstd", "n")}
              for i in range(4)]
        ln_source = [y, y, a1T, x1]

        def stepper(one):
            state = [0]

            def gs():
                one(state[0])
                state[0] += 1
            return gs

        block = ctx.enter_context(nc.Block())

        @block.sync
        def _(sp):
            def load(dst, what, key):
                sp.dma_start(dst, src[what]).then_inc(ld[key], 16)
            load(w0[:, 0:4 * P], "w0a", "w0")
            load(xF[:, 0:HT], "xFa", "x0")
            load(col[:], "col", "col")
            load(id_pack[:], "ids", "ids")
            load(bf_pack[:], "bf", "bf")
            load(w0[:, 4 * P:9 * P], "w0b", "w0b")
            load(gs_pack[:], "gs", "gs")
            load(exp_pack[:], "expert", "expert")
            load(xF[:, HT:2 * HT], "xFb", "x1")
            load(xT[:], "xT", "xT")
            load(w1[:], "w1", "w1")
            load(rows[:], "rows", "rows")
            load(w2[:], "w2", "w2")
            load(w3[:], "w3", "w3")
            stores = ((0, 0, Q), (1, 0, Q // 2), (1, Q // 2, Q))
            for t, c0, c1 in stores:
                sp.wait_ge(s["res_ready"], t * Q + c1)
                sp.dma_start(out_dram[:, t * HT + c0 * P:t * HT + c1 * P],
                             res[t][:, c0 * P:c1 * P]).then_inc(s["stored"], 16)
            sp.wait_ge(s["stored"], 16 * len(stores))

        @block.tensor
        def _(pe):
            mm = nc.tensor.matmul

            def after(free):
                for name, value in free:
                    pe.wait_ge(s[name], value)

            def keep_warm(bank, k, *free):
                after(free)
                for _ in range(k):
                    mm(bank[:], filler[:, 0:P], filler[:], start=True, stop=True)

            def gs_step(i):
                if i == 0:
                    pe.wait_ge(ld["gs"], 16)
                else:
                    pe.wait_ge(s["gs_col"], i)
                for k in range(2):
                    half = slice(k * R, (k + 1) * R)
                    j = mm(G[half, 0:P], view(ident, k * R + i, [(0, R)], k * R, R), uv[half, :],
                           start=True, stop=True)
                j.then_inc(s["gs_q"], 1)

            gs = stepper(gs_step)

            def pick_experts():
                pe.wait_ge(ld["expert"], 16)
                pe.wait_ge(s["onehot_ready"], 1)
                for o8 in range(A // Q):
                    mm(B2[:, B * o8:B * o8 + B], expw[:, o8 * P:(o8 + 1) * P], onehot[:],
                       start=True, stop=True)
                for k in range(2):
                    i = mm(B2[:, 256:256 + B], expbe[:, k * P:(k + 1) * P], onehot[:],
                           start=(k == 0), stop=(k == 1))
                i.then_inc(s["expert_picked"], 1)

            def L0_first(t, j, *free):
                k = L0_ORDER[j]
                after(free)
                if t == 0:
                    pe.wait_ge(ld["w0"], 16)
                pe.wait_ge(ld["x0" if t == 0 else "x1"], 16)
                i = mm(S_[j][:], w0[:, k * P:(k + 1) * P], xF[:, t * HT:(t + 1) * HT],
                       start=True, stop=(k > 1), skip_group_check=True)
                if k < 2:
                    pe.wait_ge(ld["bf"], 16)
                    pe.wait_ge(s["chosen_ready"], 2)
                    i = mm(S_[j][:], view(offb, k, [(0, P)], rows=3),
                           view(other, t * HB, [(1, HB), (0, S)], rows=3),
                           start=False, stop=True, skip_group_check=True)
                i.then_inc(s["pre_ready"], 1)

            def L0_second(t, *free):
                after(free)
                pe.wait_ge(ld["w0b"], 16)
                pe.wait_ge(ld["bf"], 16)
                pe.wait_ge(s["chosen_ready"], 2)
                mm(B0[:], view(offb, 2, [(0, P)], rows=3),
                   view(other, t * HB, [(1, HB), (0, S)], rows=3), start=True, stop=False,
                   skip_group_check=True)
                pe.wait_ge(s["h_ready"], 4 * t + 2)
                for k in range(2):
                    i = mm(B0[:], w0[:, (6 + k) * P:(7 + k) * P], hsr[t][:, k * HT:(k + 1) * HT],
                           start=False, stop=(k == 1), skip_group_check=True)
                i.then_inc(s["pre_z"], 1)

            def L0_third(t, *free):
                after(free)
                pe.wait_ge(ld["w0b"], 16)
                pe.wait_ge(ld["expert"], 16)
                pe.wait_ge(s["chosen_ready"], 2)
                pe.wait_ge(s["h_ready"], 4 * t + 4)
                for c in range(Q):
                    tok = slice(c * P, (c + 1) * P)
                    o = B1[:, tok]
                    mm(o, chosen[:, (t * Q + c) * P:(t * Q + c + 1) * P], b2c[:],
                       start=(c == 0), stop=False, skip_group_check=True)
                    mm(o, hnr[t][:, tok], w0[:, 4 * P:5 * P], start=False, stop=False,
                       skip_group_check=True)
                    mm(o, htsr[t][:, tok], w0[:, 5 * P:6 * P], start=False, stop=False,
                       skip_group_check=True)

            def L0_third_sr(t):
                pe.wait_ge(s["z_ready"], t + 1)
                for c in range(Q):
                    tok = slice(c * P, (c + 1) * P)
                    i = mm(B1[:, tok], zsr[t][:, tok], w0[:, 8 * P:9 * P], start=False, stop=True,
                           skip_group_check=True)
                i.then_inc(s["y0_ready"], 1)

            def to_F(what, t, *free):
                source, done, signal = {"a": (n, ln[0]["n"], "aF_pre"),
                                        "h": (n, ln[2]["n"], "hF_pre"),
                                        "c": (cT, s["ctx_ready"], "cF_pre"),
                                        "f": (n, ln[3]["n"], "fF_pre"),
                                        "o": (oT, s["o_ready"], "oF_pre")}[what]
                after(free)
                pe.wait_ge(ld["gs"], 16)
                pe.wait_ge(done, t + 1)
                for c in range(Q):
                    i = nc.tensor.transpose(B2[:, c * P:(c + 1) * P],
                                            source[t][:, c * P:(c + 1) * P], ident[:])
                i.then_inc(s[signal], 1)

            def L1_down(t, *free):
                after(free)
                if t == 0:
                    pe.wait_ge(ld["w1"], 16)
                pe.wait_ge(s["aF_ready"], t + 1)
                for c in range(Q):
                    i = mm(S_[0][c * A:(c + 1) * A, 0:P], w1[:, 0:A], aF[t][:, c * P:(c + 1) * P],
                           start=True, stop=True)
                i.then_inc(s["hid_pre"], 1)

            def L1_expert(t, *free):
                after(free)
                pe.wait_ge(s["hid_ready"], t + 1)
                if t == 0:
                    pe.wait_ge(s["expbd_ready"], 5)
                for j in range(Q):
                    sl = slice(j * S, (j + 1) * S)
                    at = (t * Q + j) * P
                    i = mm(S_[1][:, sl], expbd[:, at:at + P], hid[t][:, sl],
                           start=True, stop=True)
                i.then_inc(s["hid2_pre"], 1)

            def L1_up(t, *free):
                after(free)
                pe.wait_ge(s["hid2_ready"], t + 1)
                mm(B1[:], hid2[t][:], w1[:, A:A + Q * P], start=True, stop=True)\
                    .then_inc(s["up_ready"], 1)

            def queries(t, *free):
                after(free)
                pe.wait_ge(ld["w2"], 16)
                pe.wait_ge(s["hF_ready"], t + 1)
                mm(B0[:], w2[:, 0:P], hF[t][:], start=True, stop=True).then_inc(s["q_pre"], 1)

            def keys(t, *free):
                after(free)
                pe.wait_ge(ld["w2"], 16)
                pe.wait_ge(s["hF_ready"], t + 1)
                mm(B1[:], w2[:, P:2 * P], hF[t][:], start=True, stop=True).then_inc(s["k_pre"], 1)

            def values(t, *free):
                after(free)
                pe.wait_ge(ld["w2"], 16)
                pe.wait_ge(s["hF_ready"], t + 1)
                for b in range(HB):
                    for h in range(Q):
                        i = mm(S_[3][h * S:(h + 1) * S, b * A:(b + 1) * A],
                               hF[t][:, b * S:(b + 1) * S],
                               view(w2, 2 * P + h * DH, [(A, Q), (1, DH)]), start=True, stop=True)
                i.then_inc(s["v_pre"], 1)

            def scores(t, r, *free):
                after(free)
                pe.wait_ge(ld["bf"], 16)
                rows_ = slice(r * A, (r + 1) * A)
                mm(S_[r][:], maskl[rows_, :], view(maskr, 0, [(0, HB), (1, S)], r * A, A),
                   start=True, stop=False, skip_group_check=True)
                pe.wait_ge(s["q_split"], t + 1)
                pe.wait_ge(s["k_split"], t + 1)
                for b in range(HB):
                    qs = qbh[t][rows_, b * P:(b + 1) * P]
                    qsl = qbl[t][rows_, b * P:(b + 1) * P]
                    sl = slice(b * S, (b + 1) * S)
                    o = S_[r][:, sl]
                    mm(o, qs, kh[t][rows_, sl], start=False, stop=False, skip_group_check=True)
                    mm(o, qs, kl[t][rows_, sl], start=False, stop=False, skip_group_check=True)
                    i = mm(o, qsl, kh[t][rows_, sl], start=False, stop=(b == HB - 1),
                           skip_group_check=True)
                i.then_inc(s["s_ready"], 1)

            def subtract(t, r):
                pe.wait_ge(s["mx_ready"], 4 * t + r + 1)
                mm(S_[r][:], identb[:], view(mx[t], r * HB, [(1, HB), (0, S)]),
                   start=False, stop=True, skip_group_check=True).then_inc(s["s_sub"], 1)

            def context(t, r, *free):
                after(free)
                pe.wait_ge(s["v_ready"], t + 1)
                pe.wait_ge(s["vones_ready"], t + 1)
                pe.wait_ge(s["exT_ready"], 4 * t + r + 1)
                for b in range(HB):
                    c, j = divmod(b, Q)
                    bank = (B0, B1)[c // 2]
                    at = (c % 2) * Q * HD + r * HD
                    i = mm(bank[j * S:(j + 1) * S, at:at + HD],
                           exT[t][:, r * HT + b * S:r * HT + (b + 1) * S],
                           vbd[t][:, (b * Q + r) * HD:(b * Q + r + 1) * HD],
                           start=True, stop=True, skip_group_check=True)
                i.then_inc(s["pv_ready"], 1)

            def wo(t, *free):
                after(free)
                pe.wait_ge(s["cF_ready"], t + 1)
                for c in range(Q):
                    sl = slice(c * P, (c + 1) * P)
                    i = mm(B0[:, sl], cF[t][:, sl], w2[:, 3 * P:4 * P], start=True, stop=True)
                i.then_inc(s["wo_ready"], 1)

            def ff_in(t, k, *free):
                after(free)
                pe.wait_ge(ld["w3"], 16)
                pe.wait_ge(s["fF_ready"], t + 1)
                mm(S_[k][:], w3[:, k * P:(k + 1) * P], fF[t][:], start=True, stop=True)\
                    .then_inc(s["ff_pre"], 1)

            def ff_out(t, k, *free):
                after(free)
                pe.wait_ge(s["g_ready"], 4 * t + k + 1)
                for c in range(Q):
                    i = mm(B1[:, c * P:(c + 1) * P],
                           g[t][:, k * HT + c * P:k * HT + (c + 1) * P],
                           w3[:, (FF + k) * P:(FF + k + 1) * P],
                           start=(k == 0 and c == 0), stop=(k == FF - 1), skip_group_check=True)
                if k == FF - 1:
                    i.then_inc(s["ff_ready"], 1)

            def pool_sum(t, *free):
                after(free)
                pe.wait_ge(s["o_ready"], t + 1)
                for c in range(Q):
                    i = mm(G[:, c * Q:(c + 1) * Q], oT[t][:, c * P:(c + 1) * P], keymask,
                           start=True, stop=True)
                i.then_inc(s["pool_pre"], 1)

            def gate_hidden(t):
                pe.wait_ge(s["pooled"], t + 1)
                mm(G[0:R, 0:HB], w1[:, A + Q * P:A + Q * P + R], pool_s[t][:], start=True, stop=True)\
                    .then_inc(s["h1_pre"], 1)

            def gate_out(t):
                pe.wait_ge(s["h1_ready"], t + 1)
                for c in range(Q):
                    i = mm(G[:, c:c + 1], h1[t][:, c * P:(c + 1) * P],
                           col[0:R, COL["gate_w2"]:COL["gate_w2"] + 1], start=True, stop=True)
                i.then_inc(s["gate_pre"], 1)

            def response(t, *free):
                after(free)
                pe.wait_ge(s["oF_ready"], t + 1)
                pe.wait_ge(s["gs_mc"], 4)
                for c in range(Q):
                    sl = slice(c * P, (c + 1) * P)
                    i = mm(B0[:, sl], oF[t][:, sl], m3[:], start=True, stop=True)
                i.then_inc(s["resp_ready"], 1)

            def gs_matrix(k):
                if k == 0:
                    pe.wait_ge(s["gs_uv"], 2)
                else:
                    pe.wait_ge(s["gs_mc"], k)
                out, left, right = ((G[:, 0:P], vo, uo), (G[0:R, 0:P], uo[:, 0:R], vo),
                                    (G[:, 0:P], basisR, respw), (G[:, 0:P], basisT, t2))[k]
                mm(out, left[:], right[:], start=True, stop=True).then_inc(s["gs_m"], 1)

            pe.wait_ge(s["filler_ready"], 1)
            keep_warm(S_[0], 8)
            L0_first(0, 0)
            gs()
            L0_first(0, 1)
            L0_first(0, 2)
            L0_first(0, 3)
            gs()
            L0_second(0)
            L0_third(0)
            gs()
            L0_third_sr(0)
            L0_first(1, 0, ("h_ready", 1))
            L0_first(1, 1, ("h_ready", 2))
            gs()
            L0_first(1, 2, ("h_ready", 3))
            pick_experts()
            gs()
            L0_first(1, 3, ("h_ready", 4))
            L0_second(1, ("z_ready", 1))
            gs()
            L0_third(1, ("y0_sum", 1))
            gs()
            to_F("a", 0, ("expbd_ready", 5))
            L0_third_sr(1)
            L1_down(0, ("h_ready", 5))
            gs()
            L1_expert(0, ("h_ready", 6))
            keep_warm(B0, 1, ("z_ready", 2))
            L1_up(0, ("y0_sum", 2))
            gs()
            keep_warm(B0, 9, ("z_ready", 2))
            gs()
            to_F("a", 1, ("aF_ready", 1))
            keep_warm(S_[3], 6, ("h_ready", 8))
            gs()
            L1_down(1, ("hid_ready", 1))
            L1_expert(1, ("hid2_ready", 1))
            L1_up(1, ("y1_sum", 1))
            gs()
            keep_warm(S_[2], 5, ("h_ready", 7))
            to_F("h", 0, ("aF_ready", 2))
            gs()
            queries(0, ("z_ready", 2))
            keys(0, ("y1_sum", 2))
            gs()
            values(0, ("h_ready", 8))
            gs()
            scores(0, 0, ("hid_ready", 2))
            keep_warm(S_[2], 5, ("h_ready", 7))
            gs()
            scores(0, 1, ("hid2_ready", 2))
            scores(0, 2, ("h_ready", 7))
            gs()
            subtract(0, 0)
            scores(0, 3, ("v_ready", 1))
            to_F("h", 1, ("hF_ready", 1))
            gs()
            subtract(0, 1)
            subtract(0, 2)
            subtract(0, 3)
            queries(1, ("q_ready", 1))
            gs()
            keys(1, ("k_ready", 1))
            values(1, ("ex_ready", 4))
            gs()
            context(0, 0, ("q_ready", 2), ("k_ready", 2))
            scores(1, 0, ("ex_ready", 1))
            keep_warm(B2, 1, ("hF_ready", 2))
            gs()
            context(0, 1)
            context(0, 2)
            context(0, 3)
            gs()
            scores(1, 1, ("ex_ready", 2))
            to_F("c", 0, ("hF_ready", 2))
            gs()
            scores(1, 2, ("ex_ready", 3))
            subtract(1, 0)
            subtract(1, 1)
            gs()
            wo(0, ("ctx_ready", 1))
            scores(1, 3, ("v_ready", 2))
            gs()
            context(1, 0, ("x1_ready", 1), ("ctx_ready", 1))
            context(1, 1)
            subtract(1, 2)
            subtract(1, 3)
            keep_warm(B2, 6, ("cF_ready", 1))
            context(1, 2)
            gs()
            context(1, 3)
            keep_warm(B2, 3, ("cF_ready", 1))
            to_F("f", 0, ("cF_ready", 1))
            gs()
            keep_warm(S_[0], 2, ("ex_ready", 5))
            ff_in(0, 0, ("ex_ready", 5))
            to_F("c", 1, ("fF_ready", 1))
            ff_in(0, 1, ("ex_ready", 6))
            gs()
            wo(1, ("ctx_ready", 2))
            ff_in(0, 2, ("ex_ready", 7))
            ff_in(0, 3, ("ex_ready", 8))
            gs()
            ff_out(0, 0, ("ctx_ready", 2))
            ff_out(0, 1)
            ff_out(0, 2)
            ff_out(0, 3)
            gs()
            keep_warm(B2, 8, ("cF_ready", 2))
            to_F("f", 1, ("cF_ready", 2))
            gs()
            ff_in(1, 0, ("g_ready", 1))
            ff_in(1, 1, ("g_ready", 2))
            gs()
            ff_out(1, 0, ("u_ready", 1))
            ff_in(1, 2, ("g_ready", 3))
            to_F("o", 0, ("fF_ready", 2))
            ff_out(1, 1)
            gs_matrix(0)
            ff_in(1, 3, ("g_ready", 4))
            gs_matrix(1)
            ff_out(1, 2)
            gs_matrix(2)
            ff_out(1, 3)
            gs_matrix(3)
            pool_sum(0, ("gs_mc", 4))
            gate_hidden(0)
            response(0, ("x1_ready", 2))
            gate_out(0)
            to_F("o", 1, ("oF_ready", 1))
            pool_sum(1, ("gate_act", 1))
            response(1, ("r_ready", 1))
            gate_hidden(1)
            gate_out(1)

        @block.scalar
        def _(act):
            def c_(name, r0=0, r1=P):
                return col[r0:r1, COL[name]:COL[name] + 1]

            def gs_step(i):
                act.wait_ge(s["gs_q"], i + 1)
                nc.scalar.activation(gsq[:], G[0:2 * R, 0:P], ACT.Square,
                                     accum_out=gsn2[:, i:i + 1]).then_inc(s["gs_sq"], 1)

            gs = stepper(gs_step)

            act.wait_ge(s["filler_ready"], 1)
            for dst, cols in ((expbd, NT * Q * P), (vbd[0], HB * Q * HD), (vbd[1], HB * Q * HD)):
                nc.scalar.copy(dst[:], view(filler, 0, [(0, cols // P), (1, P)]))\
                    .then_inc(s["zeroed"], 1)

            def modulation():
                act.wait_ge(ld["col"], 16)
                nc.scalar.activation(smod[:], col[:, COL["safety0"]:COL["safety0"] + 8], ACT.Tanh,
                                     scale=0.5).then_inc(s["mod_ready"], 1)

            def L0_gelu(t, j):
                k = L0_ORDER[j]
                act.wait_ge(s["pre_ready"], 4 * t + j + 1)
                dst = (hnr[t][:], htsr[t][:], hsr[t][:, 0:HT], hsr[t][:, HT:2 * HT])[k]
                nc.scalar.activation(dst, S_[j][:], ACT.Gelu,
                                     bias=c_(("b1_nr", "b1_tsr", "b1_sr0", "b1_sr1")[k]))\
                    .then_inc(s["h_ready"], 1)

            def L0_second_gelu(t):
                act.wait_ge(s["pre_z"], t + 1)
                nc.scalar.activation(zsr[t][:], B0[:], ACT.Gelu, bias=c_("b2_sr"))\
                    .then_inc(s["z_ready"], 1)

            def evac_n(pre, ready, t, dst, gamma, beta):
                act.wait_ge(s[pre], t + 1)
                nc.scalar.activation(dst, B2[:], ACT.Identity, bias=c_(beta), scale=c_(gamma))\
                    .then_inc(s[ready], 1)

            def evac_a(t):
                evac_n("aF_pre", "aF_ready", t, aF[t][:], "gamma0", "beta0")

            def evac_h(t):
                evac_n("hF_pre", "hF_ready", t, hF[t][:], "gamma2a", "beta2a")

            def evac_f(t):
                evac_n("fF_pre", "fF_ready", t, fF[t][:], "gamma2", "beta2")

            def evac_c(t):
                act.wait_ge(s["cF_pre"], t + 1)
                nc.scalar.activation(cF[t][:], B2[:], ACT.Identity, bias=c_("bv"))\
                    .then_inc(s["cF_ready"], 1)

            def evac_o(t):
                act.wait_ge(s["oF_pre"], t + 1)
                nc.scalar.copy(oF[t][:], B2[:]).then_inc(s["oF_ready"], 1)

            def hid_gelu(t):
                act.wait_ge(s["hid_pre"], t + 1)
                nc.scalar.activation(hid[t][:], S_[0][:, 0:P], ACT.Gelu, bias=c_("down_b"))\
                    .then_inc(s["hid_ready"], 1)

            def evac_q(t):
                act.wait_ge(s["q_pre"], t + 1)
                nc.scalar.activation(q32[t][:], B0[:], ACT.Identity, bias=c_("bq"))\
                    .then_inc(s["q_ready"], 1)

            def evac_k(t):
                act.wait_ge(s["k_pre"], t + 1)
                nc.scalar.activation(k32[t][:], B1[:], ACT.Identity, bias=c_("bk"))\
                    .then_inc(s["k_ready"], 1)

            def half_q(t):
                act.wait_ge(s["q_ready"], t + 1)
                nc.scalar.copy(qh[t][:], q32[t][:]).then_inc(s["qh_ready"], 1)

            def half_k(t):
                act.wait_ge(s["k_ready"], t + 1)
                nc.scalar.copy(kh[t][:], k32[t][:]).then_inc(s["kh_ready"], 1)

            def evac_v(t):
                act.wait_ge(s["vones_ready"], t + 1)
                act.wait_ge(s["v_pre"], t + 1)
                for h in range(Q):
                    i = nc.scalar.copy(view(vbd[t], h * DH, [(HD, HB * Q), (1, DH)], h * S, S),
                                       view(S_[3], 0, [(DH, HB * Q), (1, DH)], h * S, S))
                i.then_inc(s["v_ready"], 1)

            def exps(t, r):
                act.wait_ge(s["s_sub"], 4 * t + r + 1)
                nc.scalar.activation(ex[t][:, r * HT:(r + 1) * HT], S_[r][:], ACT.Exp,
                                     scale=float(DH) ** -0.5).then_inc(s["ex_ready"], 1)

            def ff_gelu(t, k):
                act.wait_ge(s["ff_pre"], 4 * t + k + 1)
                nc.scalar.activation(g[t][:, k * HT:(k + 1) * HT], S_[k][:], ACT.Gelu,
                                     bias=c_(f"f{k}")).then_inc(s["g_ready"], 1)

            def gate_relu(t):
                act.wait_ge(s["h1_pre"], t + 1)
                nc.scalar.activation(view(h1[t], 0, [(S, HB), (1, S)], rows=R),
                                     view(G, 0, [(1, HB), (0, S)], rows=R), ACT.Relu,
                                     bias=c_("gate_b1", 0, R),
                                     scale=1.0 / S).then_inc(s["h1_ready"], 1)

            def gate_tanh(t):
                act.wait_ge(s["gate_pre"], t + 1)
                if t == 0:
                    act.wait_ge(s["gb_ready"], 1)
                nc.scalar.activation(sact[:, t * Q:(t + 1) * Q], G[:, 0:Q], ACT.Tanh,
                                     bias=gb2h[:], scale=0.5).then_inc(s["gate_act"], 1)

            modulation()
            gs()
            L0_gelu(0, 0)
            L0_gelu(0, 1)
            L0_gelu(0, 2)
            gs()
            L0_gelu(0, 3)
            L0_second_gelu(0)
            gs()
            L0_gelu(1, 0)
            gs()
            L0_gelu(1, 1)
            L0_gelu(1, 2)
            gs()
            L0_gelu(1, 3)
            gs()
            L0_second_gelu(1)
            gs()
            evac_a(0)
            hid_gelu(0)
            gs()
            gs()
            gs()
            evac_a(1)
            gs()
            hid_gelu(1)
            gs()
            evac_h(0)
            gs()
            evac_q(0)
            half_q(0)
            gs()
            evac_k(0)
            half_k(0)
            evac_v(0)
            gs()
            gs()
            gs()
            exps(0, 0)
            gs()
            evac_h(1)
            exps(0, 1)
            exps(0, 2)
            exps(0, 3)
            gs()
            evac_q(1)
            half_q(1)
            evac_k(1)
            half_k(1)
            gs()
            evac_v(1)
            gs()
            gs()
            evac_c(0)
            gs()
            exps(1, 0)
            gs()
            exps(1, 1)
            gs()
            exps(1, 2)
            exps(1, 3)
            gs()
            evac_f(0)
            gs()
            evac_c(1)
            gs()
            ff_gelu(0, 0)
            ff_gelu(0, 1)
            gs()
            ff_gelu(0, 2)
            ff_gelu(0, 3)
            gs()
            evac_f(1)
            gs()
            ff_gelu(1, 0)
            ff_gelu(1, 1)
            gs()
            ff_gelu(1, 2)
            evac_o(0)
            ff_gelu(1, 3)
            gate_relu(0)
            gate_tanh(0)
            evac_o(1)
            gate_relu(1)
            gate_tanh(1)

        @block.gpsimd
        def _(pool):
            def gs_step(i):
                pool.wait_ge(s["gs_sq"], i + 1)
                nc.gpsimd.tensor_tensor(gsn[:, i:i + 1], gsn2[:, i:i + 1], half_pos[:], ALU.pow)\
                    .then_inc(s["gs_n"], 1)
                pool.wait_ge(s["gs_n"], i + 1)
                nc.gpsimd.tensor_scalar(gsne[:, i:i + 1], gsn[:, i:i + 1], GS_EPS, None, ALU.add)\
                    .then_inc(s["gs_ne"], 1)
                pool.wait_ge(s["gs_ne"], i + 1)
                nc.gpsimd.tensor_tensor(gsr2[:, i:i + 1], gsne[:, i:i + 1], minus_two[:], ALU.pow)\
                    .then_inc(s["gs_rec"], 1)
                pool.wait_ge(s["gs_rec"], i + 1)
                pool.wait_ge(s["gs_c"], i + 1)
                nc.gpsimd.tensor_tensor(gsf[:, i:i + 1], gsc[:, i:i + 1], gsr2[:, i:i + 1],
                                        ALU.mult).then_inc(s["gs_f"], 1)

            gs = stepper(gs_step)

            def rstd_of(i, t):
                pool.wait_ge(ln[i]["mv"], t + 1)
                v = ve[:, t * Q:(t + 1) * Q]
                nc.gpsimd.tensor_scalar(v, view(mv, t * Q * 2 + 1, [(2, Q)]), EPS, None, ALU.add)\
                    .then_inc(ln[i]["ve"], 1)
                pool.wait_ge(ln[i]["ve"], t + 1)
                nc.gpsimd.tensor_tensor(rstd[:, t * Q:(t + 1) * Q], v, half_neg[:, 0:Q], ALU.pow)\
                    .then_inc(ln[i]["rstd"], 1)

            def bc(t_, i=0):
                return view(t_, i * P, [(0, Q), (1, P)])

            def q4(t_):
                return view(t_, 0, [(P, Q), (1, P)])

            def a0(t):
                pool.wait_ge(s["rowsums_ready"], 2)
                pool.wait_ge(ln[0]["n"], t + 1)
                nc.gpsimd.tensor_tensor(q4(tmp[t]), q4(n[t]), bc(rows, ROW["gamma0"]), ALU.mult)\
                    .then_inc(s["a0_tmp"], 1)
                pool.wait_ge(s["a0_tmp"], t + 1)
                nc.gpsimd.tensor_tensor(q4(a0T[t]), q4(tmp[t]), bc(b0u), ALU.add)\
                    .then_inc(s["a0T_ready"], 1)

            def a1_bo(t):
                pool.wait_ge(s["a1_ready"], t + 1)
                nc.gpsimd.tensor_tensor(q4(a1bo[t]), q4(a1T[t]), bc(rows, ROW["bo"]), ALU.add)\
                    .then_inc(s["a1bo_ready"], 1)

            def skip_sum(t):
                pool.wait_ge(s["x1_ready"], t + 1)
                nc.gpsimd.tensor_tensor(xd[t][:], x1[t][:], a1T[t][:], ALU.subtract)\
                    .then_inc(s["xd_tmp"], 1)
                pool.wait_ge(s["xd_tmp"], t + 1)
                nc.gpsimd.tensor_tensor(q4(xd[t]), q4(xd[t]), bc(rows, ROW["b2"]), ALU.add)\
                    .then_inc(s["xd_ready"], 1)

            def value_ones(t):
                pool.wait_ge(s["zeroed"], t + 2)
                pool.wait_ge(ld["col"], 16)
                nc.gpsimd.tensor_copy(view(vbd[t], A, [(HD, HB * Q), (1, Q)]),
                                      view(keymask, 0, [(0, HB * Q), (1, Q)]))\
                    .then_inc(s["vones_ready"], 1)

            def row_sums():
                pool.wait_ge(ld["col"], 16)
                nc.gpsimd.tensor_scalar(gb2h[:], col[:, COL["gate_b2"]:COL["gate_b2"] + 1], 0.5,
                                        None, ALU.mult).then_inc(s["gb_ready"], 1)
                pool.wait_ge(ld["rows"], 16)
                nc.gpsimd.tensor_tensor(b0u[:], rows[:, ROW["beta0"] * P:(ROW["beta0"] + 1) * P],
                                        rows[:, ROW["up_b"] * P:(ROW["up_b"] + 1) * P], ALU.add)\
                    .then_inc(s["rowsums_ready"], 1)
                nc.gpsimd.tensor_tensor(rsb[:], rows[:, ROW["resp_b"] * P:(ROW["resp_b"] + 1) * P],
                                        rows[:, ROW["safety_bias"] * P:
                                             (ROW["safety_bias"] + 1) * P],
                                        ALU.add).then_inc(s["rowsums_ready"], 1)

            def split_k(t):
                pool.wait_ge(s["kh_ready"], t + 1)
                nc.gpsimd.tensor_tensor(kl[t][:], k32[t][:], kh[t][:], ALU.subtract)\
                    .then_inc(s["k_split"], 1)

            nc.gpsimd.memset(half_neg[:], -0.5).then_inc(s["halves_ready"], 1)
            nc.gpsimd.memset(half_pos[:], 0.5).then_inc(s["halves_ready"], 1)
            nc.gpsimd.memset(minus_two[:], -2.0).then_inc(s["halves_ready"], 1)
            pool.wait_ge(s["halves_ready"], 3)
            value_ones(0)
            value_ones(1)
            gs()
            gs()
            row_sums()
            gs()
            gs()
            rstd_of(0, 0)
            gs()
            a0(0)
            gs()
            gs()
            gs()
            rstd_of(0, 1)
            gs()
            rstd_of(1, 0)
            gs()
            a0(1)
            gs()
            rstd_of(2, 0)
            gs()
            a1_bo(0)
            gs()
            rstd_of(1, 1)
            gs()
            split_k(0)
            gs()
            a1_bo(1)
            gs()
            rstd_of(2, 1)
            gs()
            gs()
            gs()
            split_k(1)
            gs()
            gs()
            gs()
            gs()
            gs()
            skip_sum(0)
            gs()
            rstd_of(3, 0)
            gs()
            gs()
            gs()
            skip_sum(1)
            gs()
            rstd_of(3, 1)
            gs()
            gs()
            gs()

        @block.vector
        def _(dve):
            v = nc.vector

            def gs_dot_step(i):
                dve.wait_ge(s["gs_sq"], i + 1)
                if i == 0:
                    dve.wait_ge(ld["gs"], 16)
                else:
                    dve.wait_ge(s["gs_col"], i)
                v.tensor_tensor_reduce(gsjunk[:], uv[:], G[0:2 * R, 0:P], gsneg[:, i:i + 1], 0.0,
                                       ALU.mult, ALU.add, gsc[:, i:i + 1]).then_inc(s["gs_c"], 1)

            def gs_update_step(i):
                dve.wait_ge(s["gs_f"], i + 1)
                v.scalar_tensor_tensor(uv[:], G[0:2 * R, 0:P], gsf[:, i:i + 1], uv[:],
                                       ALU.mult, ALU.add).then_inc(s["gs_col"], 1)

            gs_dot = stepper(gs_dot_step)
            gs_update = stepper(gs_update_step)

            def stats(i, t):
                source = ln_source[i][t]
                dve.wait_ge(s[("y0_sum", "y1_sum", "a1_ready", "x1_ready")[i]], t + 1)
                for c in range(Q):
                    v.bn_stats(st[:, (t * Q + c) * 6:(t * Q + c + 1) * 6],
                               source[:, c * P:(c + 1) * P]).then_inc(ln[i]["stats"], 1)
                for c in range(Q):
                    dve.wait_ge(ln[i]["stats"], Q * t + c + 1)
                    o = v.bn_aggr(mv[:, (t * Q + c) * 2:(t * Q + c + 1) * 2],
                                  st[:, (t * Q + c) * 6:(t * Q + c + 1) * 6])
                o.then_inc(ln[i]["mv"], 1)

            def apply(i, t):
                dve.wait_ge(ln[i]["rstd"], t + 1)
                dve.wait_ge(ln[i]["mv"], t + 1)
                for c in range(Q):
                    m = (t * Q + c) * 2
                    o = v.tensor_scalar(n[t][:, c * P:(c + 1) * P],
                                        ln_source[i][t][:, c * P:(c + 1) * P],
                                        mv[:, m:m + 1], rstd[:, t * Q + c:t * Q + c + 1],
                                        ALU.subtract, ALU.mult)
                o.then_inc(ln[i]["n"], 1)

            def bc(t_, i=0):
                return view(t_, i * P, [(0, Q), (1, P)])

            def q4(t_):
                return view(t_, 0, [(P, Q), (1, P)])

            v.memset(filler[:], 0.0).then_inc(s["filler_ready"], 1)

            def setup_ids():
                dve.wait_ge(ld["ids"], 16)
                v.tensor_copy(condf[:], cond_i[:]).then_inc(s["ids_step"], 1)
                v.tensor_scalar(ids[:], ids_i[:], -1.0, float(E), ALU.max, ALU.min)\
                    .then_inc(s["ids_step"], 1)
                dve.wait_ge(s["ids_step"], 2)
                dve.wait_ge(ld["col"], 16)
                v.tensor_scalar(other[:], condf[:], cidx[:], None, ALU.not_equal)\
                    .then_inc(s["chosen_ready"], 1)
                v.tensor_scalar(view(chosen, 0, [(S, B), (1, S)], rows=3),
                                view(condf, 0, [(1, B), (0, S)], rows=3), cidx[:], None,
                                ALU.is_equal).then_inc(s["chosen_ready"], 1)
                v.tensor_scalar(onehot[:], ids[:], col[0:EX, COL["expert_id"]:COL["expert_id"] + 1],
                                None, ALU.is_equal).then_inc(s["onehot_ready"], 1)

            def place_experts():
                dve.wait_ge(s["expert_picked"], 1)
                dve.wait_ge(s["zeroed"], 1)
                for c in range(Q):
                    for o4 in range(Q):
                        i = v.tensor_copy(
                            view(expbd, c * A + o4, [(Q * P, NT), (P, Q), (Q, A // Q)], c * A, A),
                            view(B2, c * Q, [(HB, NT), (1, Q), (B, A // Q)], o4 * A, A))
                    i.then_inc(s["expbd_ready"], 1)
                for c in range(Q):
                    i = v.tensor_copy(view(expb, 0, [(Q, NT), (1, Q)], c * A, A),
                                      view(B2, 256 + c * Q, [(HB, NT), (1, Q)], c * A, A))
                i.then_inc(s["expbd_ready"], 1)

            def modulation():
                dve.wait_ge(s["mod_ready"], 1)
                v.tensor_scalar(smod4[:], smod[:], 0.25, 0.25, ALU.mult, ALU.add)\
                    .then_inc(s["stren_step"], 1)

            def sum0(t):
                dve.wait_ge(s["y0_ready"], t + 1)
                if t == 0:
                    dve.wait_ge(ld["xT"], 16)
                v.tensor_tensor(y[t][:], B1[:], xT[:, t * HT:(t + 1) * HT], ALU.add)\
                    .then_inc(s["y0_sum"], 1)

            def hidden2(t):
                dve.wait_ge(s["hid2_pre"], t + 1)
                dve.wait_ge(s["expbd_ready"], 5)
                v.tensor_tensor(view(hid2[t], 0, [(S, Q), (1, S)]),
                                view(S_[1], 0, [(S, Q), (1, S)]),
                                view(expb, t * Q, [(1, Q), (0, S)]), ALU.add)\
                    .then_inc(s["hid2_ready"], 1)

            def sum1(t):
                dve.wait_ge(s["up_ready"], t + 1)
                dve.wait_ge(s["a0T_ready"], t + 1)
                v.tensor_tensor(y[t][:], B1[:], a0T[t][:], ALU.add).then_inc(s["y1_sum"], 1)

            def affine1(t):
                dve.wait_ge(ln[1]["n"], t + 1)
                if t == 0:
                    dve.wait_ge(ld["rows"], 16)
                v.tensor_tensor(q4(tmp[t]), q4(n[t]), bc(rows, ROW["gamma1"]), ALU.mult)\
                    .then_inc(s["a1_tmp"], 1)
                dve.wait_ge(s["a1_tmp"], t + 1)
                v.tensor_tensor(q4(a1T[t]), q4(tmp[t]), bc(rows, ROW["beta1"]), ALU.add)\
                    .then_inc(s["a1_ready"], 1)

            def qs_(t_):
                return view(t_, 0, [(S, HB), (1, S)])

            def split_q(t):
                dve.wait_ge(s["qh_ready"], t + 1)
                v.tensor_tensor(ql[t][:], q32[t][:], qh[t][:], ALU.subtract)\
                    .then_inc(s["ql_ready"], 1)
                for h in range(Q):
                    v.tensor_scalar(view(qbh[t], h * S, [(P, HB), (1, S)]), qs_(qh[t]),
                                    headmask[:, h:h + 1], None, ALU.mult)
                dve.wait_ge(s["ql_ready"], t + 1)
                for h in range(Q):
                    i = v.tensor_scalar(view(qbl[t], h * S, [(P, HB), (1, S)]), qs_(ql[t]),
                                        headmask[:, h:h + 1], None, ALU.mult)
                i.then_inc(s["q_split"], 1)

            def maxima(t, r):
                dve.wait_ge(s["s_ready"], 4 * t + r + 1)
                v.tensor_reduce(mx[t][:, r * HB:(r + 1) * HB], view(S_[r], 0, [(S, HB), (1, S)]),
                                AX.X, ALU.max, negate=True).then_inc(s["mx_ready"], 1)

            def turn(t, r):
                sl = slice(r * HT, (r + 1) * HT)
                dve.wait_ge(s["ex_ready"], 4 * t + r + 1)
                v.transpose(exT[t][:, sl], ex[t][:, sl]).then_inc(s["exT_ready"], 1)

            def softmax_end(t):
                dve.wait_ge(s["pv_ready"], Q * (t + 1))
                for k, bank in enumerate((B0, B1)):
                    rd = view(rden[t], k * 2 * NH, [(Q, 2 * Q), (1, Q)])
                    v.reciprocal(rd, view(bank, A, [(HD, 2 * Q), (1, Q)]))\
                        .then_inc(s["rden_ready"], 1)
                    dve.wait_ge(s["rden_ready"], 2 * t + k + 1)
                    i = v.tensor_tensor(view(cT[t], k * 2 * P, [(A, 2 * Q), (DH, Q), (1, DH)]),
                                    view(bank, 0, [(HD, 2 * Q), (DH, Q), (1, DH)]),
                                    view(rden[t], k * 2 * NH, [(Q, 2 * Q), (1, Q), (0, DH)]),
                                    ALU.mult)
                i.then_inc(s["ctx_ready"], 1)

            def sum_x1(t):
                dve.wait_ge(s["wo_ready"], t + 1)
                dve.wait_ge(s["a1bo_ready"], t + 1)
                v.tensor_tensor(x1[t][:], B0[:], a1bo[t][:], ALU.add).then_inc(s["x1_ready"], 1)

            def gated_sum(t):
                dve.wait_ge(s["ff_ready"], t + 1)
                dve.wait_ge(s["xd_ready"], t + 1)
                v.tensor_tensor(tmp[t][:], B1[:], xd[t][:], ALU.add).then_inc(s["u_ready"], 1)

            def gated(t):
                dve.wait_ge(s["u_ready"], t + 1)
                for c in range(Q):
                    sl = slice(c * P, (c + 1) * P)
                    k = COL["gate0"] + t * Q + c
                    i = v.scalar_tensor_tensor(oT[t][:, sl], tmp[t][:, sl], col[:, k:k + 1],
                                               a1T[t][:, sl], ALU.mult, ALU.add)
                i.then_inc(s["o_ready"], 1)

            def evac_pool(t):
                dve.wait_ge(s["pool_pre"], t + 1)
                v.tensor_copy(pool_s[t][:], G[:, 0:HB]).then_inc(s["pooled"], 1)

            def response_bias(t):
                dve.wait_ge(s["resp_ready"], t + 1)
                v.tensor_tensor(q4(tmp[t]), q4(B0), bc(rsb), ALU.add).then_inc(s["r_ready"], 1)

            def strength(t):
                dve.wait_ge(s["gate_act"], t + 1)
                dve.wait_ge(s["stren_step"], 1)
                sl = slice(t * Q, (t + 1) * Q)
                v.scalar_tensor_tensor(stren[:, sl], sact[:, sl], 1.0, smod4[:, sl], ALU.add,
                                       ALU.mult).then_inc(s["stren_ready"], 1)

            def final(t):
                dve.wait_ge(s["r_ready"], t + 1)
                dve.wait_ge(s["stren_ready"], t + 1)
                for c in range(Q):
                    sl = slice(c * P, (c + 1) * P)
                    k = t * Q + c
                    v.scalar_tensor_tensor(res[t][:, sl], tmp[t][:, sl], stren[:, k:k + 1],
                                           oT[t][:, sl], ALU.mult, ALU.add)\
                        .then_inc(s["res_ready"], 1)

            def gs_finish():
                v.reciprocal(gsr[:], gsne[:]).then_inc(s["gs_d"], 1)
                dve.wait_ge(s["gs_d"], 1)
                v.tensor_tensor_reduce(gsjunk[:, 0:R], gsr[:], gsdiag[:], 1.0, 0.0, ALU.mult,
                                       ALU.add, gsd[:, 0:1]).then_inc(s["gs_d"], 1)
                dve.wait_ge(s["gs_d"], 2)
                dve.wait_ge(s["gs_col"], R)
                for k, dst in enumerate((uo, vo)):
                    v.tensor_scalar(dst[:], uv[k * R:(k + 1) * R, :], gsd[k * R:(k + 1) * R, 0:1],
                                    None, ALU.mult).then_inc(s["gs_uv"], 1)

            def gs_evac(k):
                dst, n_ = ((basisT, P), (basisR, R), (t2, P), (m3, P))[k]
                dve.wait_ge(s["gs_m"], k + 1)
                v.tensor_copy(dst[:], G[0:n_, 0:P]).then_inc(s["gs_mc"], 1)

            setup_ids()
            modulation()
            gs_dot()
            gs_update()
            gs_dot()
            gs_update()
            gs_dot()
            sum0(0)
            gs_update()
            stats(0, 0)
            gs_dot()
            gs_update()
            apply(0, 0)
            gs_dot()
            gs_update()
            place_experts()
            gs_dot()
            gs_update()
            gs_dot()
            sum0(1)
            gs_update()
            stats(0, 1)
            hidden2(0)
            gs_dot()
            gs_update()
            sum1(0)
            gs_dot()
            stats(1, 0)
            gs_update()
            apply(0, 1)
            gs_dot()
            apply(1, 0)
            gs_update()
            affine1(0)
            gs_dot()
            stats(2, 0)
            hidden2(1)
            gs_update()
            sum1(1)
            gs_dot()
            apply(2, 0)
            gs_update()
            stats(1, 1)
            gs_dot()
            gs_update()
            split_q(0)
            gs_dot()
            gs_update()
            gs_dot()
            apply(1, 1)
            affine1(1)
            gs_update()
            stats(2, 1)
            gs_dot()
            maxima(0, 0)
            gs_update()
            maxima(0, 1)
            apply(2, 1)
            gs_dot()
            maxima(0, 2)
            gs_update()
            maxima(0, 3)
            gs_dot()
            turn(0, 0)
            turn(0, 1)
            gs_update()
            turn(0, 2)
            gs_dot()
            turn(0, 3)
            gs_update()
            split_q(1)
            gs_dot()
            gs_update()
            gs_dot()
            maxima(1, 0)
            gs_update()
            softmax_end(0)
            gs_dot()
            gs_update()
            gs_dot()
            maxima(1, 1)
            gs_update()
            turn(1, 0)
            gs_dot()
            maxima(1, 2)
            sum_x1(0)
            gs_update()
            turn(1, 1)
            maxima(1, 3)
            gs_dot()
            stats(3, 0)
            turn(1, 2)
            turn(1, 3)
            gs_update()
            gs_dot()
            apply(3, 0)
            gs_update()
            softmax_end(1)
            gs_dot()
            gs_update()
            gs_dot()
            sum_x1(1)
            gs_update()
            stats(3, 1)
            gs_dot()
            gs_update()
            gated_sum(0)
            gs_dot()
            apply(3, 1)
            gs_update()
            gs_dot()
            gated(0)
            gs_update()
            gs_dot()
            gs_update()
            gs_finish()
            gs_evac(0)
            gs_evac(1)
            gs_evac(2)
            gs_evac(3)
            gated_sum(1)
            evac_pool(0)
            gated(1)
            response_bias(0)
            strength(0)
            final(0)
            evac_pool(1)
            response_bias(1)
            strength(1)
            final(1)


_OUT = "out_0_dram"


def layout(i):
    f = {k.replace("_cond_", "_"): np.asarray(v) for k, v in i.items()}
    c = np.ascontiguousarray
    x = f["x"].reshape(8, P, P)
    xF = x.reshape(8 * P, P).T
    xT = x.transpose(1, 0, 2).reshape(P, 8 * P)
    out = {}
    out["xFa"], out["xFb"] = c(xF[:, :HT]), c(xF[:, HT:])
    out["xT"] = c(xT)
    out["w0a"] = c(np.concatenate([f["L0_w1_nr"], f["L0_w1_tsr"], f["L0_w1_sr"]], 1))
    out["w0b"] = c(np.concatenate([f["L0_w2_nr"], f["L0_w2_tsr"], f["L0_w2_sr"][:P],
                                   f["L0_w2_sr"][P:], f["L0_w3_sr"]], 1))
    up = np.zeros((Q, A, Q, P), np.float32)
    for q in range(Q):
        up[q, :, q] = f["L1_up_W"].T
    out["w1"] = c(np.concatenate([f["L1_down_W"].T, up.reshape(P, Q * P), f["L3_gate_w1"].T], 1))
    out["w2"] = c(np.concatenate([f[f"L2_W{k}"] for k in "qkvo"], 1))
    w2 = f["L2_W2"].reshape(FF, P, P).transpose(1, 0, 2).reshape(P, FF * P)
    out["w3"] = c(np.concatenate([f["L2_W1"], w2], 1))

    def tokens(a):
        return np.repeat(a.reshape(8, Q), S, axis=1).T

    def padded(a, fill=0.0):
        return np.concatenate([a, np.full(P - len(a), fill, np.float32)])

    cols = {"b1_nr": f["L0_b1_nr"], "b1_tsr": f["L0_b1_tsr"], "b1_sr0": f["L0_b1_sr"][:P],
            "b1_sr1": f["L0_b1_sr"][P:], "b2_sr": f["L0_b2_sr"], "gamma0": f["L0_gamma"],
            "beta0": f["L0_beta"], "down_b": np.tile(f["L1_down_b"], Q),
            "gamma2a": f["L2_gamma1"], "beta2a": f["L2_beta1"], "bq": f["L2_bq"],
            "bk": f["L2_bk"], "bv": f["L2_bv"], "gamma2": f["L2_gamma2"], "beta2": f["L2_beta2"],
            "gate_b1": padded(f["L3_gate_b1"]), "gate_w2": padded(f["L3_gate_w2"][0]),
            "gate_b2": np.repeat(f["L3_gate_b2"], P),
            "expert_id": padded(np.array([*range(E), E, -1], np.float32))}
    cols |= {f"f{k}": f["L2_b1"][k * P:(k + 1) * P] for k in range(FF)}
    cols |= {f"gate{k}": tokens(f["condB_gatescore"])[:, k] for k in range(8)}
    cols |= {f"safety{k}": tokens(f["condB_safetyscore"])[:, k] for k in range(8)}
    p = np.arange(P)
    cols |= {f"head{h}": ((p % A) // DH == h).astype(np.float32) for h in range(Q)}
    cols |= {f"quad{h}": (p // A == h).astype(np.float32) for h in range(Q)}
    cols["branch"] = p.astype(np.float32)
    out["col"] = c(np.stack([cols[k] for k in COLS], 1))
    rows = {"gamma0": "L0_gamma", "beta0": "L0_beta", "up_b": "L1_up_b", "gamma1": "L1_ln_gamma",
            "beta1": "L1_ln_beta", "bo": "L2_bo", "b2": "L2_b2", "resp_b": "L3_resp_b",
            "safety_bias": "L3_safety_bias"}
    out["rows"] = c(np.broadcast_to(np.concatenate([f[rows[k]] for k in ROWS]), (P, len(ROWS) * P)))
    eye = np.eye(A, dtype=np.float32).reshape(1, A * A)
    none = np.zeros((2, A), np.float32)
    emb = f["L1_domain_emb"]
    expert = np.zeros((R, A * A + 4 * P), np.float32)
    expert[:EX, :A * A] = np.concatenate([f["L1_expert_W"].reshape(E, A * A), eye, eye], 0)
    expert[:EX, A * A:A * A + P] = np.tile(np.concatenate([f["L1_expert_b"], none], 0), Q)
    expert[:EX, A * A + P:A * A + 2 * P] = np.tile(np.concatenate([emb, emb[-1:], emb[:1]], 0), Q)
    expert[:3, A * A + 2 * P:A * A + 3 * P] = [f["L0_b2_nr"], f["L0_b2_tsr"], f["L0_b3_sr"]]
    expert[:, A * A + 3 * P:] = f["L3_resp_w"].T
    out["expert"] = expert
    ids = np.concatenate([f["itok_B_0_15"], f["itok_B_0_2"]])
    out["ids"] = c(np.broadcast_to(ids, (EX, 2 * B)))
    gs = np.zeros((P, 2 * P + 2 * R), np.float32)
    p64 = np.arange(2 * R)[:, None] % R
    gs[:, :P] = np.eye(P)
    gs[:2 * R, P:2 * P] = np.concatenate([f["L3_U"].T, f["L3_V"].T], 0)
    gs[:2 * R, 2 * P:2 * P + R] = -(p64 > np.arange(R)[None]).astype(np.float32)
    gs[:2 * R, 2 * P + R:] = p64 == np.arange(R)[None]
    out["gs"] = gs
    bf = np.zeros((P, 2 * P + S + 3), np.float32)
    bf[:, :P] = np.eye(P)
    bf[:, P:2 * P] = p[:, None] % S == p[None] % S
    bf[:, 2 * P:2 * P + S] = np.where(np.arange(S)[None] > p[:, None] % S, MASKED, 0.0)
    bf[:3, 2 * P + S:] = np.eye(3) * OFF
    out["bf"] = bf.astype(np.dtype("bfloat16"))
    return out


def kernel(**inputs):
    import concourse.bacc as bacc
    from concourse.bass_utils import run_bass_kernel_spmd

    nc = bacc.Bacc("TRN2", target_bir_lowering=False, num_devices=1)
    arrays = layout(inputs)
    src = {k: nc.dram_tensor("in_" + k, a.shape, mybir.dt.from_np(a.dtype), kind="ExternalInput").ap()
           for k, a in arrays.items()}
    out = nc.dram_tensor(_OUT, (P, 8 * P), F32, kind="ExternalOutput").ap()
    build(nc, src, out)
    r = run_bass_kernel_spmd(nc, [{"in_" + k: a for k, a in arrays.items()}], core_ids=[0])
    got = r.results[0][_OUT].reshape(P, 8, P)
    return np.ascontiguousarray(got.transpose(1, 0, 2)).reshape(B, S, P)
```
